# Optimizing a Trainium2 kernel written in Bass

```python
import numpy as np
import jax
import jax.numpy as jnp

def _softmax(x, axis=-1):
    return jax.nn.softmax(x, axis=axis)

def _gelu(x):
    return jax.nn.gelu(x, approximate=True)

def _silu(x):
    return jax.nn.silu(x)

def _sigmoid(x):
    return jax.nn.sigmoid(x)

def _layernorm(x, axis=-1, eps=1e-05):
    m = jnp.mean(x, axis=axis, keepdims=True)
    v = jnp.var(x, axis=axis, keepdims=True)
    return (x - m) / jnp.sqrt(v + eps)

def _scatter_add(tgt, idx, src, axis=0):
    return tgt.at[idx].add(src)

def _segment_sum(src, seg, n):
    return jax.ops.segment_sum(src, seg, n)
kernel_name = 'mk_adaln_d1_jaxref_r8_6af81f'

def setup_inputs(seed: int=0):
    np.random.seed(seed)
    _w = jnp.asarray

    def _L0_attn_setup():
        import jax, jax.numpy as jnp
        import numpy as np
        import math
        N_EMBD = 256
        N_HEADS = 16
        HEAD_DIM = N_EMBD // N_HEADS
        CTX = 256

        def alibi_bias(seq_len: int, n_heads: int) -> jnp.ndarray:
            i = jnp.arange(seq_len)[:, None]
            j = jnp.arange(seq_len)[None, :]
            pos = jnp.where(j <= i, (j - i).astype(jnp.float32), 0.0)
            slopes = 2.0 ** (-8.0 / jnp.arange(1, n_heads + 1, dtype=jnp.float32))
            return slopes[:, None, None] * pos[None, :, :]

        def causal_mask(seq_len: int) -> jnp.ndarray:
            i = jnp.arange(seq_len)[:, None]
            j = jnp.arange(seq_len)[None, :]
            return jnp.where(j > i, -jnp.inf, 0.0).astype(jnp.float32)
        key = jax.random.key(seed)
        k_x, k_qkv, k_o = jax.random.split(key, 3)
        scale = 1.0 / math.sqrt(N_EMBD)
        x = jax.random.normal(k_x, (2, CTX, N_EMBD), dtype=jnp.float32)
        W_qkv = jax.random.normal(k_qkv, (N_EMBD, 3 * N_EMBD), dtype=jnp.float32) * scale
        W_o = jax.random.normal(k_o, (N_EMBD, N_EMBD), dtype=jnp.float32) * scale
        return {'x': x, 'W_qkv': W_qkv, 'W_o': W_o}
    _L0_attn_in = _L0_attn_setup()

    def _L0_ffn_setup():
        import jax, jax.numpy as jnp
        import numpy as np
        B, S, H = (4, 256, 256)
        E = 8
        F = H // E
        TOPK = 2
        LORA_R = 16
        LORA_SCALE = 1.0
        key = jax.random.key(seed)
        ks = jax.random.split(key, 7)
        x = jax.random.normal(ks[0], (B, S, H), dtype=jnp.float32)
        G = jax.random.normal(ks[1], (H, E), dtype=jnp.float32)
        gate_w = jax.random.normal(ks[2], (E, F, H), dtype=jnp.float32) * np.float32(np.sqrt(2.0 / H))
        up_w = jax.random.normal(ks[3], (E, F, H), dtype=jnp.float32) * np.float32(np.sqrt(2.0 / H))
        down_w = jax.random.normal(ks[4], (E, H, F), dtype=jnp.float32) * np.float32(np.sqrt(2.0 / F))
        lora_A = jax.random.normal(ks[5], (E, LORA_R, H), dtype=jnp.float32) * np.float32(np.sqrt(2.0 / H))
        lora_B = jax.random.normal(ks[6], (E, H, LORA_R), dtype=jnp.float32) * np.float32(np.sqrt(2.0 / LORA_R))
        return {'x': x, 'G': G, 'gate_w': gate_w, 'up_w': up_w, 'down_w': down_w, 'lora_A': lora_A, 'lora_B': lora_B}
    _L0_ffn_in = _L0_ffn_setup()
    _L0_c = _w((lambda *s: np.random.randn(*s).astype(np.float32) * 0.05)(1, 256))
    _L0_wmod = _w((lambda *s: np.random.randn(*s).astype(np.float32) * 0.05)(256, 6 * 256) * 256 ** (-0.5))
    _d = {'L0_attn_x': _L0_attn_in['x'], 'L0_attn_W_qkv': _L0_attn_in['W_qkv'], 'L0_attn_W_o': _L0_attn_in['W_o'], 'L0_ffn_G': _L0_ffn_in['G'], 'L0_ffn_gate_w': _L0_ffn_in['gate_w'], 'L0_ffn_up_w': _L0_ffn_in['up_w'], 'L0_ffn_down_w': _L0_ffn_in['down_w'], 'L0_ffn_lora_A': _L0_ffn_in['lora_A'], 'L0_ffn_lora_B': _L0_ffn_in['lora_B'], 'L0_c': _L0_c, 'L0_wmod': _L0_wmod}
    _x0 = _d['L0_attn_x']
    _d['L0_attn_x'] = jax.random.normal(jax.random.fold_in(jax.random.key(seed), 1), (1, 2048, 256), dtype=_x0.dtype)
    del _x0
    return _d

def reference(L0_attn_x, L0_attn_W_qkv, L0_attn_W_o, L0_ffn_G, L0_ffn_gate_w, L0_ffn_up_w, L0_ffn_down_w, L0_ffn_lora_A, L0_ffn_lora_B, L0_c, L0_wmod):

    def _L0_attn_ref(x, W_qkv, W_o):
        import jax, jax.numpy as jnp
        import numpy as np
        import math
        N_EMBD = 256
        N_HEADS = 16
        HEAD_DIM = N_EMBD // N_HEADS
        CTX = 256

        def alibi_bias(seq_len: int, n_heads: int) -> jnp.ndarray:
            i = jnp.arange(seq_len)[:, None]
            j = jnp.arange(seq_len)[None, :]
            pos = jnp.where(j <= i, (j - i).astype(jnp.float32), 0.0)
            slopes = 2.0 ** (-8.0 / jnp.arange(1, n_heads + 1, dtype=jnp.float32))
            return slopes[:, None, None] * pos[None, :, :]

        def causal_mask(seq_len: int) -> jnp.ndarray:
            i = jnp.arange(seq_len)[:, None]
            j = jnp.arange(seq_len)[None, :]
            return jnp.where(j > i, -jnp.inf, 0.0).astype(jnp.float32)
        bsz, seq_len, n_embd = x.shape
        qkv = jnp.einsum('bsd,de->bse', x, W_qkv)
        q, k, v = jnp.split(qkv, 3, axis=-1)

        def to_heads(t):
            return t.reshape(bsz, seq_len, N_HEADS, HEAD_DIM).transpose(0, 2, 1, 3)
        q, k, v = (to_heads(q), to_heads(k), to_heads(v))
        attn = jnp.einsum('bhqd,bhkd->bhqk', q, k) / math.sqrt(HEAD_DIM)
        attn = attn + alibi_bias(seq_len, N_HEADS)[None] + causal_mask(seq_len)[None, None]
        attn = jax.nn.softmax(attn, axis=-1)
        y = jnp.einsum('bhqk,bhkd->bhqd', attn, v)
        y = y.transpose(0, 2, 1, 3).reshape(bsz, seq_len, n_embd)
        return jnp.einsum('bsd,de->bse', y, W_o)

    def _L0_ffn_ref(x, G, gate_w, up_w, down_w, lora_A, lora_B):
        import jax, jax.numpy as jnp
        import numpy as np
        B, S, H = (4, 256, 256)
        E = 8
        F = H // E
        TOPK = 2
        LORA_R = 16
        LORA_SCALE = 1.0
        scores = jax.nn.softmax(jnp.einsum('bsh,he->bse', x, G), axis=-1)
        value, indices = jax.lax.top_k(scores, TOPK)
        onehot = jax.nn.one_hot(indices, E, dtype=value.dtype)
        w = jnp.einsum('bsk,bske->bse', value, onehot)
        gate = jax.nn.silu(jnp.einsum('bsh,efh->bsef', x, gate_w))
        up = jnp.einsum('bsh,efh->bsef', x, up_w)
        gated = gate * up
        out = jnp.einsum('bsef,bse,ehf->bsh', gated, w, down_w)
        lr = jnp.einsum('bsh,erh->bser', x, lora_A)
        out = out + LORA_SCALE * jnp.einsum('bser,bse,ehr->bsh', lr, w, lora_B)
        return out
    x = L0_attn_x
    mod = (_silu(L0_c) @ L0_wmod).reshape(L0_c.shape[0], 6, 1, -1)
    sa, ca, ga, sb, cb, gb = (mod[:, 0], mod[:, 1], mod[:, 2], mod[:, 3], mod[:, 4], mod[:, 5])
    ga = (2 * (ga >= 0) - 1) * jnp.maximum(jnp.abs(ga), 0.25)
    gb = (2 * (gb >= 0) - 1) * jnp.maximum(jnp.abs(gb), 0.25)
    h = _layernorm(x, axis=-1) * (1 + ca) + sa
    x = x + ga * _L0_attn_ref(h, L0_attn_W_qkv, L0_attn_W_o)
    h = _layernorm(x, axis=-1) * (1 + cb) + sb
    x = x + gb * _L0_ffn_ref(h, L0_ffn_G, L0_ffn_gate_w, L0_ffn_up_w, L0_ffn_down_w, L0_ffn_lora_A, L0_ffn_lora_B)
    return x

_drawn_inputs = setup_inputs


def setup_inputs(seed=0):
    import zlib

    import numpy as np

    out = dict(_drawn_inputs(seed))
    spreads = {}
    factors = {}
    for name, (base, spread) in spreads.items():
        noise = np.random.default_rng([zlib.crc32(name.encode()), seed]).standard_normal(out[name].shape)
        drawn = base * np.exp(spread * noise) if base else spread * noise
        out[name] = jnp.asarray(drawn.astype(out[name].dtype))
    for name, factor in factors.items():
        out[name] = (out[name] * factor).astype(out[name].dtype)
    return out
```

```python
import numpy as np
import concourse.bass as bass
from concourse import mybir
from contextlib import ExitStack


SEQ, DM, HEADS, HD = 2048, 256, 16, 16
TOK = 128
TILE = 512
TILES = SEQ // TILE
SUBS = TILE // TOK
HPI = HEADS // SUBS
CH = DM // 128
EXPERTS, FF, RANK = 8, 32, 16
GU = 2 * EXPERTS * FF
LORA = EXPERTS * RANK
LR = LORA + EXPERTS
DOWN = (EXPERTS * FF + LORA) // 128
EPS = 1e-5

PARTS = 3
PAIRS = [(0, 0), (0, 1), (1, 0), (0, 2), (2, 0), (1, 1)]
ROW_QK = 4 * PARTS
ROW_SHIFT = ROW_QK + len(PAIRS) * HD
ROW_END = ROW_SHIFT + PARTS
VC = PARTS * HD + 1
MASKED = -1e30

CHUNK = 2 * TILE
PRING, LRING = 8, 4
LAG = 4
SPLIT_ON_VECTOR = [set(), set(), {2}, {0, 2, 4, 6}]
SCALE = 1.0 / HD ** 0.5


def chunks_of(t):
    return 2 * t + 2


def chunk_blocks(t, j):
    if j < 2 * t:
        return [(2 * j, 0, 0, 0, TILE), (2 * j + 1, 0, 1, 0, TILE)]
    k = SUBS * t
    if j == 2 * t:
        return [(k, 0, 0, 0, 512), (k + 1, 1, 1, 0, 384), (k + 3, 3, 1, 384, 128)]
    return [(k + 2, 2, 0, 0, 256)]


def chunk_width(t, j):
    return CHUNK if j <= 2 * t else 256


def chunks_before(t):
    return HEADS * sum(chunks_of(i) for i in range(t))


def maxes_before(t):
    return HEADS * SUBS * sum(i + 1 for i in range(t))


def splits_before(t, j, vector):
    return sum((i in SPLIT_ON_VECTOR[t]) == vector for i in range(j))


def all_splits_before(t, vector):
    return HEADS * sum(splits_before(i, chunks_of(i), vector) for i in range(t))


FFN_STEPS = ["y", "yT", "proj", "norm", "hT", "route", "select", "gate", "gated", "gT", "down", "out"]


def turn(attend, scan, feed):
    n = HPI * chunks_of(attend) if attend is not None else 0
    slots = n + LAG if n else 12
    scans = HPI * SUBS * (scan + 1) if scan is not None else 0
    steps, done, fed = [], 0, 0
    for i in range(slots):
        if i < n:
            steps.append(("scores", i))
        if 1 <= i <= n:
            steps.append(("split", i - 1))
        while done * slots < scans * (i + 1) and done < scans:
            steps.append(("scan", done))
            done += 1
        while feed is not None and fed * slots < len(FFN_STEPS) * (i + 1) and fed < len(FFN_STEPS):
            steps.append((FFN_STEPS[fed], 0))
            fed += 1
        if n and i >= LAG:
            steps.append(("mix", i - LAG))
    if scan is not None:
        steps.append(("shift", 0))
    return steps


STAGES = ([(None, 0, None)]
          + [(t, t + 1 if t + 1 < TILES else None, t - 1 if t else None) for t in range(TILES)]
          + [(None, None, TILES - 1)])

FFN_LINKS = 14
SHIFT_LINKS = 5


def decoder_layer(nc, x, c_cols, wmod, wqkv, wo, w_lr, w_gu, w_down, alibi_k, alibi_q, ident,
                  mask_q, mask_k, out):
    f32, bf16, f16 = mybir.dt.float32, mybir.dt.bfloat16, mybir.dt.float16
    ALU, ACT, AX = mybir.AluOpType, mybir.ActivationFunctionType, mybir.AxisListType

    x_t = x.rearrange("(t s p) d -> t p s d", s=SUBS, p=TOK)
    scratch = nc.dram_tensor("qk_parts", [2, PARTS, DM, SEQ], bf16, kind="Internal").ap()

    ctx = ExitStack()
    with ctx:
        def sb(name, shape, dt):
            return ctx.enter_context(nc.sbuf_tensor(name, shape, dt))

        def sem(name):
            return ctx.enter_context(nc.semaphore(name))

        loop_sems = []

        def loop_sem(name):
            loop_sems.append(sem(name))
            return loop_sems[-1]

        ka = sb("ka", [128, HEADS, SEQ], bf16)
        qa = sb("qa", [128, 2, HEADS, TILE], bf16)
        vp = sb("vp", [128, SEQ // TOK, HEADS, VC], bf16)
        probs = sb("probs", [128, PRING, CHUNK], f32)
        probs_lo = sb("probs_lo", [128, LRING, CHUNK], f16)
        yraw = sb("yraw", [128, 2, SUBS, HEADS, VC], f32)
        wo_sb = sb("wo_sb", [128, CH, DM], f32)
        w_lr_sb = sb("w_lr_sb", [128, CH, LR], f32)
        w_gu_sb = sb("w_gu_sb", [128, CH, GU], f32)
        w_down_sb = sb("w_down_sb", [128, DOWN, DM], f32)
        idf = sb("idf", [128, 128], f32)
        idb = sb("idb", [128, 128], bf16)
        mask_q_sb = sb("mask_q_sb", [128, 128], bf16)
        mask_k_sb = sb("mask_k_sb", [128, 128], bf16)
        xd = sb("xd", [128, DM], f32)
        yn = sb("yn", [128, DM], f32)
        tT = sb("tT", [128, CH, TOK], f32)
        g = sb("g", [128, EXPERTS * FF + LORA], f32)
        gT = sb("gT", [128, DOWN, TOK], f32)
        res = sb("res", [128, DM], f32)
        rden = sb("rden", [128, HEADS], f32)
        stats = sb("stats", [128, SUBS, 6], f32)
        mv = sb("mv", [128, SUBS, 2], f32)
        ve = sb("ve", [128, SUBS], f32)
        rstd = sb("rstd", [128, SUBS], f32)
        minus_half = sb("minus_half", [128, SUBS], f32)
        modc = sb("modc", [128, 4, CH], f32)
        silc = sb("silc", [128, 4, CH], f32)
        e16 = sb("e16", [128, 2 * EXPERTS], f32)
        left = sb("left", [128, 2 * EXPERTS], f32)
        top8 = sb("top8", [128, 8], f32)
        top2 = sb("top2", [128, 8], f32)
        rsm = sb("rsm", [128, 4], f32)
        wexp = sb("wexp", [128, 3, EXPERTS], f32)
        part_max = sb("part_max", [128, HPI * SUBS, TILES], f32)
        neg_max = sb("neg_max", [128, 3, HPI * SUBS], f32)
        shift = sb("shift", [128, 128], bf16)
        shift_rows = sb("shift_rows", [PARTS * HPI * SUBS, TOK], bf16)

        ring = probs[:, :, :].rearrange("p a b -> p (a b)")
        wqkv_sb = ring[:, 0:1536].rearrange("p (c e) -> p c e", c=CH)
        xin = ring[:, 1536:3584].rearrange("p (b s d) -> p b s d", b=2, s=SUBS)
        hT = ring[:, 3584:5632].rearrange("p (b c t) -> p b c t", b=2, c=CH)
        resid = ring[:, 5632:7680].rearrange("p (b t) -> p b t", b=4)
        nrm = ring[:, 7680:8192].rearrange("p (b d) -> p b d", b=2)
        parts = probs_lo[:, :, :].rearrange("p a b -> p (a b)").bitcast(bf16)[:, 0:3072] \
            .rearrange("p (b a t) -> p b a t", b=2, a=PARTS)
        raw = yraw[:, :, :, :, :].rearrange("p a b c d -> p (a b c d)")
        wmod_sb = raw[:, 0:3072].rearrange("p (c e) -> p c e", c=CH)
        silb = raw[:, 3072:3328].rearrange("p (c t) -> p c t", c=CH)
        gates = raw[:, 3328:4352].rearrange("p (a e) -> p a e", a=2)

        bank = ctx.enter_context(nc.psum_tensor("bank", [128, 8, 512], f32))
        st = [bank[:, 2 * b:2 * b + 2, :].rearrange("p a b -> p (a b)") for b in range(2)]
        SCAN, MIX, MISC = 4, 6, 7

        w_mod = sem("w_mod")
        w_in = sem("w_in")
        w_rest = sem("w_rest")
        consts = sem("consts")
        made = sem("made")
        fill = sem("fill")
        x_in = [sem(f"x_in{b}") for b in range(2)]
        own = sem("own")
        sil_th = sem("sil_th")
        sil_ready = sem("sil_ready")
        mod_psum = sem("mod_psum")
        mod_ready = sem("mod_ready")
        var1 = sem("var1")
        rstd1 = sem("rstd1")
        n1 = sem("n1")
        hT_psum = sem("hT_psum")
        hT_ready = sem("hT_ready")
        qk_psum = sem("qk_psum")
        qk_hi = sem("qk_hi")
        qk_mid = sem("qk_mid")
        qk_lo = sem("qk_lo")
        v_psum = sem("v_psum")
        v_hi = sem("v_hi")
        v_mid = sem("v_mid")
        v_lo = sem("v_lo")
        stored = [sem(f"stored{b}") for b in range(2)]
        k_rows = [sem(f"k_rows{t}") for t in range(TILES)]
        q_rows = [sem(f"q_rows{t}") for t in range(TILES)]
        scan_psum = loop_sem("scan_psum")
        scan_max = loop_sem("scan_max")
        shift_own = loop_sem("shift_own")
        shift_parts = loop_sem("shift_parts")
        shift_psum = loop_sem("shift_psum")
        shift_sb = loop_sem("shift_sb")
        shift_in = loop_sem("shift_in")
        scores_psum = loop_sem("scores_psum")
        exp_done = loop_sem("exp_done")
        split_v = loop_sem("split_v")
        split_g = loop_sem("split_g")
        mixed = loop_sem("mixed")
        y_out = loop_sem("y_out")
        xd_in = loop_sem("xd_in")
        ffn_own = loop_sem("ffn_own")
        y_ready = loop_sem("y_ready")
        yT_psum = loop_sem("yT_psum")
        yT_ready = loop_sem("yT_ready")
        proj_psum = loop_sem("proj_psum")
        x1_var = loop_sem("x1_var")
        rstd2 = loop_sem("rstd2")
        n2 = loop_sem("n2")
        n2T_psum = loop_sem("n2T_psum")
        h2T_ready = loop_sem("h2T_ready")
        route_psum = loop_sem("route_psum")
        route_max = loop_sem("route_max")
        route_exp = loop_sem("route_exp")
        lora_done = loop_sem("lora_done")
        gu_psum = loop_sem("gu_psum")
        tanh_done = loop_sem("tanh_done")
        gated = loop_sem("gated")
        gT_psum = loop_sem("gT_psum")
        gT_ready = loop_sem("gT_ready")
        down_psum = loop_sem("down_psum")
        res_ready = loop_sem("res_ready")
        res_out = loop_sem("res_out")
        unread = sem("unread")

        def wait_alone(engine, semaphore, value):
            engine.wait_ge(semaphore, value)
            engine.sem_inc(unread, 1)

        def pair(a):
            return a.rearrange("p (s h d) -> p s h d", s=2, d=HD)

        def v_part(n, a):
            return vp[:, 2 * n:2 * n + 2, :, HD * a:HD * (a + 1)]

        def at(base, per_turn, u, k):
            return u * per_turn + (base + k + 1)

        block = ctx.enter_context(nc.Block())

        @block.sync
        def _(sp):
            sp.dma_start(silc[:, 0, :], c_cols).then_inc(w_mod, 16)
            sp.dma_start(xin[:, 0, :, :], x_t[0]).then_inc(x_in[0], 16)
            sp.dma_start(idf[:, :], ident).then_inc(consts, 16)
            sp.dma_start(wmod_sb, wmod).then_inc(w_mod, 16)
            sp.dma_start(wqkv_sb, wqkv).then_inc(w_in, 16)
            sp.dma_start(xin[:, 1, :, :], x_t[1]).then_inc(x_in[1], 16)
            sp.dma_start(mask_q_sb[:, :], mask_q).then_inc(consts, 16)
            sp.dma_start(mask_k_sb[:, :], mask_k).then_inc(consts, 16)
            sp.dma_start(ka[0:ROW_QK, :, :], alibi_k[0:ROW_QK]).then_inc(fill, 16)
            sp.dma_start(ka[ROW_SHIFT:ROW_END, :, :], alibi_k[ROW_QK:ROW_QK + PARTS]).then_inc(fill, 16)
            sp.dma_start(wo_sb[:, :, :], wo).then_inc(w_rest, 16)
            sp.dma_start(w_down_sb[:, :, :], w_down).then_inc(w_rest, 16)
            sp.dma_start(w_lr_sb[:, :, :], w_lr).then_inc(w_rest, 16)
            sp.dma_start(w_gu_sb[:, :, :], w_gu).then_inc(w_rest, 16)
            for t in range(TILES):
                for j in range(2 * CH):
                    n = 2 * CH * t + j
                    sp.wait_ge(qk_lo, n + 1)
                    sp.dma_start(
                        scratch[j // CH, :, 128 * (j % CH):128 * (j % CH + 1), TILE * t:TILE * (t + 1)]
                        .rearrange("a p t -> p a t"), parts[:, n % 2, :, :]).then_inc(stored[n % 2], 16)
                if t + 2 < TILES:
                    sp.wait_ge(n1, SUBS * (t + 1))
                    sp.dma_start(xin[:, t % 2, :, :], x_t[t + 2]).then_inc(x_in[t % 2], 16)
                for b in range(2):
                    sp.wait_ge(stored[b], 16 * CH * (t + 1))
                for i, (pq, pk) in enumerate(PAIRS):
                    rows = slice(ROW_QK + HD * i, ROW_QK + HD * (i + 1))
                    sp.dma_start(ka[rows, :, TILE * t:TILE * (t + 1)],
                                 scratch[1, pk, :, TILE * t:TILE * (t + 1)]
                                 .rearrange("(h d) t -> d h t", d=HD)).then_inc(k_rows[t], 16)
                    if t < 2:
                        sp.dma_start(qa[rows, t, :, :],
                                     scratch[0, pq, :, TILE * t:TILE * (t + 1)]
                                     .rearrange("(h d) t -> d h t", d=HD)).then_inc(q_rows[t], 16)
                if t < 2:
                    sp.dma_start(qa[0:ROW_QK, t, :, :],
                                 alibi_q[:, :, TILE * t:TILE * (t + 1)]).then_inc(q_rows[t], 16)

            def shift_load(t, u):
                wait_alone(sp, shift_sb, at(SUBS * t, 1, u, 1))
                for p in range(PARTS):
                    sp.dma_start(
                        qa[ROW_SHIFT + p:ROW_SHIFT + p + 1, t % 2, bass.ds(u * HPI, HPI), :],
                        shift_rows[HPI * SUBS * p:HPI * SUBS * (p + 1), :]).then_inc(shift_in, 16)
                wait_alone(sp, shift_in, at(16 * PARTS * SUBS * t, 16 * PARTS, u, 16 * PARTS))

            for attend, scan, feed in STAGES:
                with sp.Fori(0, SUBS) as u:
                    if feed is not None:
                        wait_alone(sp, res_ready, at(SUBS * feed, 1, u, 0))
                        sp.dma_start(xd[:, :], x[bass.ds(u * TOK + feed * TILE, TOK), :]).then_inc(xd_in, 16)
                    if feed is not None:
                        wait_alone(sp, res_ready, at(SUBS * feed, 1, u, 1))
                        sp.dma_start(out[bass.ds(u * TOK + feed * TILE, TOK), :], res[:, :]).then_inc(res_out, 16)
                        wait_alone(sp, res_out, at(16 * SUBS * feed, 16, u, 16))
                    if scan is not None:
                        shift_load(scan, u)
                    if attend is not None and attend + 2 < TILES:
                        t = attend + 2
                        wait_alone(sp, scores_psum, at(chunks_before(attend), HPI * chunks_of(attend), u,
                                                   HPI * chunks_of(attend)))
                        for i, (pq, _) in enumerate(PAIRS):
                            sp.dma_start(qa[ROW_QK + HD * i:ROW_QK + HD * (i + 1), t % 2, bass.ds(u * HPI, HPI), :],
                                         scratch[0, pq, bass.ds(u * HPI * HD, HPI * HD), TILE * t:TILE * (t + 1)]
                                         .rearrange("(h d) t -> d h t", d=HD)).then_inc(q_rows[t], 16)
                        sp.dma_start(qa[0:ROW_QK, t % 2, bass.ds(u * HPI, HPI), :],
                                     alibi_q[:, bass.ds(u * HPI, HPI), TILE * t:TILE * (t + 1)])\
                            .then_inc(q_rows[t], 16)
            sp.wait_ge(res_out, at(16 * SUBS * TILES, 0, 0, 0))

        @block.gpsimd
        def _(pool):
            for s in loop_sems:
                pool.sem_inc(s, 1)
            pool.memset(minus_half[:, :], -0.5).then_inc(made, 1)
            pool.memset(e16[:, :], -1.0).then_inc(made, 1)
            pool.memset(top2[:, :], -1.0).then_inc(made, 1)
            pool.memset(shift[:, :], 0.0).then_inc(made, 1)
            pool.memset(vp[:, :, :, VC - 1:VC], 1.0).then_inc(made, 1)
            def inverse_std(t):
                pool.wait_ge(var1, t + 1)
                pool.tensor_tensor(rstd[:, :], ve[:, :], minus_half[:, :], ALU.pow).then_inc(rstd1, 1)

            pool.wait_ge(made, 5)
            inverse_std(0)
            for t in range(TILES):
                for j in range(2 * CH):
                    n = 2 * CH * t + j
                    pool.wait_ge(qk_mid, n + 1)
                    pool.tensor_tensor(parts[:, n % 2, 2, :], resid[:, j % 2, :], parts[:, n % 2, 1, :],
                                       ALU.subtract).then_inc(qk_lo, 1)
                if t + 1 < TILES:
                    inverse_std(t + 1)
                for b in range(2):
                    n = 2 * t + b
                    pool.wait_ge(v_mid, n + 1)
                    pool.tensor_tensor(v_part(n, 2), pair(resid[:, 2 + b, :]), v_part(n, 1),
                                       ALU.subtract).then_inc(v_lo, 1)
            for attend, scan, feed in STAGES:
                with pool.Fori(0, SUBS) as u:
                    for step, i in turn(attend, scan, feed):
                        if step == "split":
                            t, nc_ = attend, chunks_of(attend)
                            hh, j = i // nc_, i % nc_
                            if j in SPLIT_ON_VECTOR[t]:
                                continue
                            w = chunk_width(t, j)
                            pool.wait_ge(exp_done, at(chunks_before(t), HPI * nc_, u, i + 1))
                            if t or i >= LRING:
                                pool.wait_ge(mixed, at(chunks_before(t), HPI * nc_, u, i + 1 - LRING))
                            else:
                                pool.wait_ge(mixed, at(0, HPI * nc_, u, 0))
                            p = probs[:, i % PRING, 0:w]
                            pool.tensor_tensor(probs_lo[:, i % LRING, 0:w], p, p.bitcast(bf16)[:, 1::2],
                                               ALU.subtract).then_inc(split_g, 1)
                        elif step == "norm":
                            pool.wait_ge(x1_var, at(SUBS * feed, 1, u, 1))
                            pool.tensor_tensor(rstd[:, 0:1], ve[:, 0:1], minus_half[:, 0:1],
                                               ALU.pow).then_inc(rstd2, 1)

        @block.scalar
        def _(act):
            act.wait_ge(w_mod, 32)
            act.activation(silc[:, 1, :], silc[:, 0, :], ACT.Tanh, scale=0.5).then_inc(sil_th, 1)
            for t in range(TILES):
                act.wait_ge(hT_psum, SUBS * (t + 1))
                if t == 0:
                    act.wait_ge(mod_ready, 1)
                for c in range(CH):
                    if t >= 2 and c == 0:
                        act.wait_ge(v_psum, 2 * (t - 1))
                    act.activation(hT[:, t % 2, c, :], bank[:, c, :], ACT.Identity,
                                   scale=modc[:, 0, c:c + 1], bias=modc[:, 1, c:c + 1]).then_inc(hT_ready, 1)
                for j in range(2 * CH):
                    n = 2 * CH * t + j
                    act.wait_ge(qk_psum, n + 1)
                    if n >= 2:
                        act.wait_ge(stored[n % 2], 16 * (n // 2))
                    act.activation(parts[:, n % 2, 0, :], bank[:, 2 + j, :], ACT.Copy).then_inc(qk_hi, 1)
                for b in range(2):
                    n = 2 * t + b
                    act.wait_ge(v_psum, n + 1)
                    act.activation(v_part(n, 0), pair(bank[:, 6 + b, :]), ACT.Copy).then_inc(v_hi, 1)
            act.wait_ge(v_lo, 2 * TILES)
            act.wait_ge(mod_ready, 2)
            for attend, scan, feed in STAGES:
                with act.Fori(0, SUBS) as u:
                    for step, i in turn(attend, scan, feed):
                        if step == "scores":
                            t, nc_ = attend, chunks_of(attend)
                            j = i % nc_
                            w = chunk_width(t, j)
                            if t or i >= PRING:
                                act.wait_ge(mixed, at(chunks_before(t), HPI * nc_, u, i + 1 - PRING))
                            else:
                                act.wait_ge(mixed, at(0, HPI * nc_, u, 0))
                            act.wait_ge(scores_psum, at(chunks_before(t), HPI * nc_, u, i + 1))
                            act.activation(probs[:, i % PRING, 0:w], st[i % 2][:, 0:w], ACT.Exp,
                                           scale=SCALE).then_inc(exp_done, 1)
                        elif step == "mix" and (i + 1) % chunks_of(attend) == 0:
                            t, nc_ = attend, chunks_of(attend)
                            hh = i // nc_
                            act.wait_ge(mixed, at(chunks_before(t), HPI * nc_, u, i + 1))
                            act.activation(yraw[:, t % 2, :, u * HPI + hh, :],
                                           bank[:, MIX, 0:SUBS * VC].rearrange("p (s v) -> p s v", v=VC),
                                           ACT.Copy).then_inc(y_out, 1)
                        elif step == "yT":
                            act.wait_ge(yT_psum, at(SUBS * feed, 1, u, 1))
                            act.activation(tT[:, :, :].rearrange("p c t -> p (c t)"), bank[:, MISC, 0:DM],
                                           ACT.Copy).then_inc(yT_ready, 1)
                        elif step == "hT":
                            act.wait_ge(n2T_psum, at(SUBS * feed, 1, u, 1))
                            for c in range(CH):
                                act.activation(tT[:, c, :], bank[:, MISC, TOK * c:TOK * (c + 1)], ACT.Identity,
                                               scale=modc[:, 2, c:c + 1], bias=modc[:, 3, c:c + 1])\
                                    .then_inc(h2T_ready, 1)
                        elif step == "route":
                            act.wait_ge(route_max, at(SUBS * feed, 1, u, 1))
                            act.activation(e16[:, 0:EXPERTS], bank[:, MISC, LORA:LR], ACT.Exp,
                                           bias=rsm[:, 0:1], accum_out=rsm[:, 1:2]).then_inc(route_exp, 1)
                        elif step == "gate":
                            act.wait_ge(gu_psum, at(SUBS * feed, 1, u, 1))
                            act.activation(g[:, 0:EXPERTS * FF], bank[:, MISC, 0:EXPERTS * FF], ACT.Tanh,
                                           scale=0.5).then_inc(tanh_done, 1)
                        elif step == "gT":
                            act.wait_ge(gT_psum, at(SUBS * feed, 1, u, 1))
                            act.activation(gT[:, :, :].rearrange("p c t -> p (c t)"),
                                           bank[:, MISC, 0:DOWN * TOK], ACT.Copy).then_inc(gT_ready, 1)
                        elif step == "shift":
                            act.wait_ge(shift_psum, at(SUBS * scan, 1, u, 1))
                            act.wait_ge(shift_in, at(16 * PARTS * SUBS * scan, 16 * PARTS, u, 0))
                            act.activation(shift_rows[:, :],
                                           bank[0:PARTS * HPI * SUBS, MISC, 0:TOK // 2].bitcast(bf16),
                                           ACT.Copy).then_inc(shift_sb, 1)

        @block.vector
        def _(dve):
            links = [0]

            def link(ins):
                links[0] += 1
                ins.then_inc(own, 1)
                dve.wait_ge(own, links[0])

            dve.wait_ge(sil_th, 1)
            link(dve.scalar_tensor_tensor(out=silc[:, 2, :], in0=silc[:, 1, :], scalar=1.0, in1=silc[:, 0, :],
                                          op0=ALU.add, op1=ALU.mult))
            link(dve.tensor_scalar(silc[:, 3, :], silc[:, 2, :], 0.5, None, ALU.mult))
            link(dve.memset(silb, 1.0))
            for c in range(CH):
                ins = dve.tensor_scalar(silb[:, c, :], silb[:, c, :], silc[:, 3, c:c + 1], None, ALU.mult)
            ins.then_inc(sil_ready, 1)

            def norm_tile(t):
                dve.wait_ge(x_in[t % 2], 16 * (t // 2 + 1))
                for s in range(SUBS):
                    ins = dve.bn_stats(stats[:, s, :], xin[:, t % 2, s, :])
                link(ins)
                for s in range(SUBS):
                    ins = dve.bn_aggr(mv[:, s, :], stats[:, s, :])
                link(ins)
                dve.tensor_scalar(ve[:, :], mv[:, :, 1], EPS, None, ALU.add).then_inc(var1, 1)
                dve.wait_ge(rstd1, t + 1)
                for s in range(SUBS):
                    n = SUBS * t + s
                    if n >= 2:
                        dve.wait_ge(hT_psum, n - 1)
                    dve.tensor_scalar(nrm[:, n % 2, :], xin[:, t % 2, s, :], mv[:, s, 0:1], rstd[:, s:s + 1],
                                      ALU.subtract, ALU.mult).then_inc(n1, 1)

            norm_tile(0)
            dve.wait_ge(mod_psum, 1)
            cols = bank[:, 7, 0:8].rearrange("p (m c) -> p m c", c=CH)
            link(dve.tensor_copy(modc[:, 1:4:2, :], cols[:, 0:4:2, :]))
            dve.tensor_scalar(modc[:, 0:3:2, :], cols[:, 1:4:2, :], 1.0, None, ALU.add).then_inc(mod_ready, 1)
            link(dve.tensor_scalar(gates[:, 0, :], bank[:, 6, :], 0.0, 2.0, ALU.is_ge, ALU.mult))
            link(dve.scalar_tensor_tensor(out=gates[:, 1, :], in0=gates[:, 0, :], scalar=-1.0,
                                          in1=bank[:, 6, :], op0=ALU.add, op1=ALU.mult))
            link(dve.tensor_scalar(gates[:, 1, :], gates[:, 1, :], 0.25, None, ALU.max))
            link(dve.scalar_tensor_tensor(out=gates[:, 0, :], in0=gates[:, 0, :], scalar=-1.0,
                                          in1=gates[:, 1, :], op0=ALU.add, op1=ALU.mult))
            dve.wait_ge(w_rest, 64)
            for w_sb, n, a in ((wo_sb, CH, 0), (w_down_sb, DOWN, DM)):
                for c in range(n):
                    ins = dve.tensor_tensor(w_sb[:, c, :], w_sb[:, c, :], gates[:, 0, a:a + DM], ALU.mult)
            ins.then_inc(mod_ready, 1)
            dve.wait_ge(consts, 48)
            dve.tensor_copy(idb[:, :], idf[:, :]).then_inc(mod_ready, 1)
            for t in range(TILES):
                for j in range(2 * CH):
                    n = 2 * CH * t + j
                    dve.wait_ge(qk_hi, n + 1)
                    if n >= 2:
                        dve.wait_ge(qk_lo, n - 1)
                    link(dve.tensor_tensor(resid[:, j % 2, :], bank[:, 2 + j, :], parts[:, n % 2, 0, :],
                                           ALU.subtract))
                    dve.tensor_copy(parts[:, n % 2, 1, :], resid[:, j % 2, :]).then_inc(qk_mid, 1)
                if t + 1 < TILES:
                    norm_tile(t + 1)
                for b in range(2):
                    n = 2 * t + b
                    dve.wait_ge(v_hi, n + 1)
                    if n >= 2:
                        dve.wait_ge(v_lo, n - 1)
                    r = pair(resid[:, 2 + b, :])
                    link(dve.tensor_tensor(r, pair(bank[:, 6 + b, :]), v_part(n, 0), ALU.subtract))
                    dve.tensor_copy(v_part(n, 1), r).then_inc(v_mid, 1)
            dve.wait_ge(made, 5)

            for attend, scan, feed in STAGES:
                with dve.Fori(0, SUBS) as u:
                    k = [0]

                    def ffn_link(ins, wait=dve.wait_ge):
                        k[0] += 1
                        ins.then_inc(ffn_own, 1)
                        wait(ffn_own, at(FFN_LINKS * SUBS * feed, FFN_LINKS, u, k[0]))

                    def alone(semaphore, value):
                        wait_alone(dve, semaphore, value)

                    for step, i in turn(attend, scan, feed):
                        if step == "scan":
                            r, c = (i // (scan + 1)), i % (scan + 1)
                            w = TILE if c < scan else TOK * (r % SUBS + 1)
                            dve.wait_ge(scan_psum, at(maxes_before(scan), HPI * SUBS * (scan + 1), u, i + 1))
                            dve.tensor_reduce(part_max[:, r, c:c + 1], bank[:, SCAN + i % 2, 0:w], AX.X,
                                              ALU.max).then_inc(scan_max, 1)
                        elif step == "shift":
                            kk = [0]

                            def shift_link(ins):
                                kk[0] += 1
                                ins.then_inc(shift_own, 1)
                                dve.wait_ge(shift_own, at(SHIFT_LINKS * SUBS * scan, SHIFT_LINKS, u, kk[0]))

                            dve.wait_ge(scan_max, at(maxes_before(scan), HPI * SUBS * (scan + 1), u,
                                                     HPI * SUBS * (scan + 1)))
                            shift_link(dve.tensor_reduce(neg_max[:, 0, :], part_max[:, :, 0:scan + 1], AX.X,
                                                         ALU.max, negate=True))
                            n = HPI * SUBS
                            dve.wait_ge(shift_psum, at(SUBS * scan, 1, u, 0))
                            shift_link(dve.tensor_copy(shift[:, 0:n], neg_max[:, 0, :]))
                            shift_link(dve.tensor_tensor(neg_max[:, 1, :], neg_max[:, 0, :], shift[:, 0:n],
                                                         ALU.subtract))
                            shift_link(dve.tensor_copy(shift[:, n:2 * n], neg_max[:, 1, :]))
                            shift_link(dve.tensor_tensor(shift[:, 2 * n:3 * n], neg_max[:, 1, :],
                                                         shift[:, n:2 * n], ALU.subtract))
                            assert kk[0] == SHIFT_LINKS
                        elif step == "split":
                            t, nc_ = attend, chunks_of(attend)
                            j = i % nc_
                            if j not in SPLIT_ON_VECTOR[t]:
                                continue
                            w = chunk_width(t, j)
                            dve.wait_ge(exp_done, at(chunks_before(t), HPI * nc_, u, i + 1))
                            dve.wait_ge(mixed, at(chunks_before(t), HPI * nc_, u, i + 1 - LRING))
                            p = probs[:, i % PRING, 0:w]
                            dve.tensor_tensor(probs_lo[:, i % LRING, 0:w], p, p.bitcast(bf16)[:, 1::2],
                                              ALU.subtract).then_inc(split_v, 1)
                        elif step == "y":
                            dve.wait_ge(y_out, at(HEADS * (feed + 1), 0, 0, 0))
                            ys = yraw[:, feed % 2, u, :, :]
                            dve.reciprocal(rden[:, :], ys[:, :, VC - 1])
                            ffn_link(dve.tensor_reduce(
                                yn[:, :].rearrange("p (h d) -> p h d", d=HD),
                                ys[:, :, 0:VC - 1].rearrange("p h (a d) -> p h d a", a=PARTS), AX.X, ALU.add))
                            yh = yn[:, :].rearrange("p (h d) -> p h d", d=HD)
                            dve.tensor_tensor(yh, yh, rden[:, :].unsqueeze(2).broadcast_to((128, HEADS, HD)),
                                              ALU.mult).then_inc(y_ready, 1)
                        elif step == "proj":
                            dve.wait_ge(xd_in, at(16 * SUBS * feed, 16, u, 16))
                            dve.wait_ge(proj_psum, at(SUBS * feed, 1, u, 1))
                            ffn_link(dve.tensor_tensor(xd[:, :], bank[:, MISC, 0:DM], xd[:, :], ALU.add))
                            ffn_link(dve.bn_stats(stats[:, 0, :], xd[:, :]), alone)
                            ffn_link(dve.bn_aggr(mv[:, 0, :], stats[:, 0, :]))
                            dve.tensor_scalar(ve[:, 0:1], mv[:, 0, 1:2], EPS, None, ALU.add).then_inc(x1_var, 1)
                        elif step == "norm":
                            dve.wait_ge(rstd2, at(SUBS * feed, 1, u, 1))
                            dve.tensor_scalar(yn[:, :], xd[:, :], mv[:, 0, 0:1], rstd[:, 0:1],
                                              ALU.subtract, ALU.mult).then_inc(n2, 1)
                        elif step == "route":
                            dve.wait_ge(route_psum, at(SUBS * feed, 1, u, 1))
                            dve.tensor_reduce(rsm[:, 0:1], bank[:, MISC, LORA:LR], AX.X, ALU.max,
                                              negate=True).then_inc(route_max, 1)
                        elif step == "select":
                            dve.wait_ge(route_exp, at(SUBS * feed, 1, u, 1))
                            dve.reciprocal(rsm[:, 2:3], rsm[:, 1:2])
                            ffn_link(dve.max(top8[:, :], e16[:, 0:EXPERTS]))
                            ffn_link(dve.tensor_copy(top2[:, 0:2], top8[:, 0:2]))
                            ffn_link(dve.tensor_scalar(rsm[:, 3:4], rsm[:, 2:3], 0.5, None, ALU.mult), alone)
                            ffn_link(dve.match_replace(out=left[:, :], in_to_replace=top2[:, :],
                                                       in_values=e16[:, :], imm_value=0.0))
                            ffn_link(dve.tensor_tensor(wexp[:, 0, :], e16[:, 0:EXPERTS], left[:, 0:EXPERTS],
                                                       ALU.subtract))
                            dve.tensor_scalar(wexp[:, 1, :], wexp[:, 0, :], rsm[:, 2:3], None, ALU.mult)
                            ffn_link(dve.tensor_scalar(wexp[:, 2, :], wexp[:, 0, :], rsm[:, 3:4], None, ALU.mult))
                            dve.tensor_tensor(
                                g[:, EXPERTS * FF:].rearrange("p (e r) -> p e r", r=RANK),
                                bank[:, MISC, 0:LORA].rearrange("p (e r) -> p e r", r=RANK),
                                wexp[:, 1, :].unsqueeze(2).broadcast_to((128, EXPERTS, RANK)),
                                ALU.mult).then_inc(lora_done, 1)
                        elif step == "gated":
                            gg = g[:, 0:EXPERTS * FF]
                            dve.wait_ge(tanh_done, at(SUBS * feed, 1, u, 1))
                            ffn_link(dve.scalar_tensor_tensor(out=gg, in0=gg, scalar=1.0,
                                                              in1=bank[:, MISC, 0:EXPERTS * FF],
                                                              op0=ALU.add, op1=ALU.mult))
                            ffn_link(dve.tensor_tensor(gg, bank[:, MISC, EXPERTS * FF:GU], gg, ALU.mult))
                            ge = gg.rearrange("p (e f) -> p e f", f=FF)
                            ffn_link(dve.tensor_tensor(
                                ge, ge, wexp[:, 2, :].unsqueeze(2).broadcast_to((128, EXPERTS, FF)), ALU.mult))
                        elif step == "out":
                            dve.wait_ge(down_psum, at(SUBS * feed, 1, u, 1))
                            dve.wait_ge(res_out, at(16 * SUBS * feed, 16, u, 0))
                            ffn_link(dve.tensor_tensor(res[:, :], bank[:, MISC, 0:DM], xd[:, :], ALU.add))
                            dve.tensor_copy(rsm[:, 0:1], rsm[:, 0:1]).then_inc(res_ready, 1)
                    assert feed is None or k[0] == FFN_LINKS, k[0]

        @block.tensor
        def _(pe):
            pe.wait_ge(sil_ready, 1)
            for m, vec in enumerate((0, 1, 3, 4)):
                for c in range(CH):
                    for k in range(CH):
                        pe.matmul(bank[:, 7, CH * m + c:CH * m + c + 1],
                                  wmod_sb[:, k, DM * vec + 128 * c:DM * vec + 128 * (c + 1)],
                                  silc[:, 3, k:k + 1], start=(k == 0), stop=(k == CH - 1))
            for m, vec in enumerate((2, 5)):
                for k in range(CH):
                    ins = pe.matmul(bank[:, 6, DM * m:DM * (m + 1)], silb[:, k, :],
                                    wmod_sb[:, k, DM * vec:DM * (vec + 1)], start=(k == 0), stop=(k == CH - 1))
            ins.then_inc(mod_psum, 1)
            pe.wait_ge(consts, 48)
            for t in range(TILES):
                for s in range(SUBS):
                    n = SUBS * t + s
                    pe.wait_ge(n1, n + 1)
                    if t and s == 0:
                        pe.wait_ge(hT_ready, CH * t)
                    for c in range(CH):
                        ins = pe.transpose(bank[:, c, TOK * s:TOK * (s + 1)], nrm[:, n % 2, 128 * c:128 * (c + 1)],
                                           idf[:, :])
                    ins.then_inc(hT_psum, 1)
                pe.wait_ge(hT_ready, CH * (t + 1))
                if t == 0:
                    pe.wait_ge(w_in, 16)
                for j in range(2 * CH):
                    if t:
                        pe.wait_ge(qk_mid, 2 * CH * (t - 1) + j + 1)
                    for k in range(CH):
                        ins = pe.matmul(bank[:, 2 + j, :], wqkv_sb[:, k, 128 * j:128 * (j + 1)],
                                        hT[:, t % 2, k, :], start=(k == 0), stop=(k == CH - 1))
                    ins.then_inc(qk_psum, 1)
                for s in range(SUBS):
                    if t == 0 and s == 0:
                        pe.wait_ge(mod_ready, 2)
                    if t and s % 2 == 0:
                        pe.wait_ge(v_mid, 2 * (t - 1) + s // 2 + 1)
                    for k in range(CH):
                        ins = pe.matmul(bank[:, 6 + s // 2, DM * (s % 2):DM * (s % 2 + 1)],
                                        hT[:, t % 2, k, TOK * s:TOK * (s + 1)],
                                        wqkv_sb[:, k, 2 * DM:3 * DM], start=(k == 0), stop=(k == CH - 1))
                    if s % 2:
                        ins.then_inc(v_psum, 1)
            pe.wait_ge(qk_mid, 2 * CH * TILES)
            pe.wait_ge(v_lo, 2 * TILES)
            pe.wait_ge(mod_ready, 3)
            pe.wait_ge(fill, 32)
            pe.wait_ge(made, 5)

            for attend, scan, feed in STAGES:
                if scan is not None:
                    pe.wait_ge(k_rows[scan], 16 * len(PAIRS))
                    pe.wait_ge(q_rows[scan], 16 * (len(PAIRS) + 1) * (1 if scan < 2 else SUBS))
                with pe.Fori(0, SUBS) as u:
                    for step, i in turn(attend, scan, feed):
                        if step == "scores":
                            t, nc_ = attend, chunks_of(attend)
                            hh, j = i // nc_, i % nc_
                            h = u * HPI + hh
                            if i == 0:
                                pe.wait_ge(shift_in, at(16 * PARTS * SUBS * t, 16 * PARTS, u, 16 * PARTS))
                            if t or i >= 2:
                                pe.wait_ge(exp_done, at(chunks_before(t), HPI * nc_, u, i - 1))
                            else:
                                pe.wait_ge(exp_done, at(0, HPI * nc_, u, 0))
                            for kb, sub, b, col, w in chunk_blocks(t, j):
                                o = bank[:, 2 * (i % 2) + b, col:col + w]
                                diag = kb >= SUBS * t
                                if diag:
                                    pe.matmul(o[:, 0:TOK], idb[:, :], mask_k_sb[:, :],
                                              start=True, stop=False, skip_group_check=True)
                                ins = pe.matmul(o, ka[0:ROW_END, h, TOK * kb:TOK * (kb + 1)],
                                                qa[0:ROW_END, t % 2, h, TOK * sub:TOK * sub + w],
                                                start=not diag, stop=True, skip_group_check=diag)
                            ins.then_inc(scores_psum, 1)
                        elif step == "mix":
                            t, nc_ = attend, chunks_of(attend)
                            hh, j = i // nc_, i % nc_
                            h = u * HPI + hh
                            if j == 0:
                                pe.wait_ge(y_out, at(HEADS * t, HPI, u, hh))
                            for low in range(2):
                                if low:
                                    vector = j in SPLIT_ON_VECTOR[t]
                                    per = splits_before(t, nc_, vector)
                                    pe.wait_ge(split_v if vector else split_g,
                                               at(all_splits_before(t, vector), HPI * per, u,
                                                  hh * per + splits_before(t, j, vector) + 1))
                                elif i >= 0:
                                    pe.wait_ge(exp_done, at(chunks_before(t), HPI * nc_, u, i + 1))
                                for kb, sub, b, col, w in chunk_blocks(t, j):
                                    for q in range(w // TOK):
                                        a = TILE * b + col + TOK * q
                                        if low:
                                            p = probs_lo[:, i % LRING, a:a + TOK]
                                        else:
                                            p = probs[:, i % PRING, a:a + TOK].bitcast(bf16)[:, 1::2]
                                        s = sub + q
                                        ins = pe.matmul(bank[:, MIX, VC * s:VC * (s + 1)], p, vp[:, kb, h, :],
                                                        start=(j == 0 and not low and kb == 0 and s == 0),
                                                        stop=bool(low) and kb == SUBS * t + min(s, 2),
                                                        skip_group_check=True)
                            ins.then_inc(mixed, 1)
                        elif step == "scan":
                            r, c = i // (scan + 1), i % (scan + 1)
                            h, s = u * HPI + r // SUBS, r % SUBS
                            w = TILE if c < scan else TOK * (s + 1)
                            if scan or i >= 2:
                                pe.wait_ge(scan_max, at(maxes_before(scan), HPI * SUBS * (scan + 1), u, i - 1))
                            else:
                                pe.wait_ge(scan_max, at(0, HPI * SUBS * (scan + 1), u, 0))
                            o = bank[:, SCAN + i % 2, :]
                            diag = c == scan
                            if diag:
                                pe.matmul(o[:, w - TOK:w], idb[:, :], mask_q_sb[:, :],
                                          start=True, stop=False, skip_group_check=True)
                            pe.matmul(o[:, 0:w], qa[0:ROW_SHIFT, scan % 2, h, TOK * s:TOK * (s + 1)],
                                      ka[0:ROW_SHIFT, h, TILE * c:TILE * c + w],
                                      start=not diag, stop=True, skip_group_check=diag).then_inc(scan_psum, 1)
                        elif step == "shift":
                            pe.wait_ge(shift_own, at(SHIFT_LINKS * SUBS * scan, SHIFT_LINKS, u, SHIFT_LINKS))
                            if feed is not None:
                                pe.wait_ge(res_ready, at(SUBS * feed, 1, u, 1))
                            else:
                                pe.wait_ge(shift_sb, at(SUBS * scan, 1, u, 0))
                            pe.transpose(bank[:, MISC, 0:TOK // 2].bitcast(bf16), shift[:, :],
                                         idb[:, :]).then_inc(shift_psum, 1)
                        elif step == "yT":
                            pe.wait_ge(y_ready, at(SUBS * feed, 1, u, 1))
                            if scan is not None:
                                pe.wait_ge(shift_sb, at(SUBS * scan, 1, u, 0))
                            else:
                                pe.wait_ge(shift_sb, at(SUBS * TILES, 0, 0, 0))
                                pe.wait_ge(res_ready, at(SUBS * feed, 1, u, 0))
                            for c in range(CH):
                                ins = pe.transpose(bank[:, MISC, TOK * c:TOK * (c + 1)],
                                                   yn[:, 128 * c:128 * (c + 1)], idf[:, :])
                            ins.then_inc(yT_psum, 1)
                        elif step == "proj":
                            pe.wait_ge(yT_ready, at(SUBS * feed, 1, u, 1))
                            for c in range(CH):
                                ins = pe.matmul(bank[:, MISC, 0:DM], tT[:, c, :], wo_sb[:, c, :],
                                                start=(c == 0), stop=(c == CH - 1))
                            ins.then_inc(proj_psum, 1)
                        elif step == "hT":
                            pe.wait_ge(n2, at(SUBS * feed, 1, u, 1))
                            for c in range(CH):
                                ins = pe.transpose(bank[:, MISC, TOK * c:TOK * (c + 1)],
                                                   yn[:, 128 * c:128 * (c + 1)], idf[:, :])
                            ins.then_inc(n2T_psum, 1)
                        elif step == "route":
                            pe.wait_ge(h2T_ready, at(CH * SUBS * feed, CH, u, CH))
                            for c in range(CH):
                                ins = pe.matmul(bank[:, MISC, 0:LR], tT[:, c, :], w_lr_sb[:, c, :],
                                                start=(c == 0), stop=(c == CH - 1))
                            ins.then_inc(route_psum, 1)
                        elif step == "gate":
                            pe.wait_ge(lora_done, at(SUBS * feed, 1, u, 1))
                            for c in range(CH):
                                ins = pe.matmul(bank[:, MISC, 0:GU], tT[:, c, :], w_gu_sb[:, c, :],
                                                start=(c == 0), stop=(c == CH - 1))
                            ins.then_inc(gu_psum, 1)
                        elif step == "gT":
                            pe.wait_ge(ffn_own, at(FFN_LINKS * SUBS * feed, FFN_LINKS, u, FFN_LINKS - 1))
                            for c in range(DOWN):
                                ins = pe.transpose(bank[:, MISC, TOK * c:TOK * (c + 1)],
                                                   g[:, 128 * c:128 * (c + 1)], idf[:, :])
                            ins.then_inc(gT_psum, 1)
                        elif step == "down":
                            pe.wait_ge(gT_ready, at(SUBS * feed, 1, u, 1))
                            for c in range(DOWN):
                                ins = pe.matmul(bank[:, MISC, 0:DM], gT[:, c, :], w_down_sb[:, c, :],
                                                start=(c == 0), stop=(c == DOWN - 1))
                            ins.then_inc(down_psum, 1)


def constants():
    bf = np.dtype("bfloat16")
    slopes = np.float32(2.0) ** (np.float32(-8.0) / np.arange(1, HEADS + 1, dtype=np.float32))
    rest, slope_parts = slopes * np.float32(HD ** 0.5), []
    for _ in range(PARTS):
        part = rest.astype(bf).astype(np.float32)
        slope_parts.append(part)
        rest = rest - part
    pos = np.arange(SEQ)
    high, low = (pos // TOK * TOK).astype(np.float32), (pos % TOK).astype(np.float32)
    ones = np.ones(SEQ, np.float32)
    k_side, q_side = [], []
    for part in slope_parts:
        for at_key, at_query, sign in ((high, ones, 1), (ones, high, -1), (low, ones, 1), (ones, low, -1)):
            if sign > 0:
                k_side.append(np.broadcast_to(at_key, (HEADS, SEQ)))
                q_side.append(part[:, None] * ones[None, :])
            else:
                k_side.append(-part[:, None] * ones[None, :])
                q_side.append(np.broadcast_to(at_query, (HEADS, SEQ)))
    k_side += [np.ones((HEADS, SEQ), np.float32)] * PARTS
    i = np.arange(TOK)
    return {
        "alibi_k": np.stack(k_side).astype(bf),
        "alibi_q": np.stack(q_side).astype(bf),
        "ident": np.eye(TOK, dtype=np.float32),
        "mask_q": np.where(i[None, :] > i[:, None], MASKED, 0.0).astype(bf),
        "mask_k": np.where(i[:, None] > i[None, :], MASKED, 0.0).astype(bf),
    }


def kernel(L0_attn_x, L0_attn_W_qkv, L0_attn_W_o, L0_ffn_G, L0_ffn_gate_w, L0_ffn_up_w, L0_ffn_down_w,
           L0_ffn_lora_A, L0_ffn_lora_B, L0_c, L0_wmod):
    import concourse.bacc as _bacc
    from concourse.bass_utils import run_bass_kernel_spmd as _run

    def rows(w):
        w = np.asarray(w)
        return np.ascontiguousarray(w.reshape(-1, 128, w.shape[-1]).transpose(1, 0, 2))

    def by_input(w):
        w = np.asarray(w)
        return w.reshape(-1, w.shape[-1]).T

    def by_feature(w):
        w = np.asarray(w)
        return w.transpose(0, 2, 1).reshape(-1, w.shape[1])

    arrays = {
        "x": np.ascontiguousarray(np.asarray(L0_attn_x).reshape(SEQ, DM)),
        "c_cols": np.ascontiguousarray(np.asarray(L0_c).reshape(CH, 128).T),
        "wmod": rows(L0_wmod),
        "wqkv": rows(L0_attn_W_qkv),
        "wo": rows(L0_attn_W_o),
        "w_lr": rows(np.concatenate([by_input(L0_ffn_lora_A), np.asarray(L0_ffn_G)], axis=1)),
        "w_gu": rows(np.concatenate([by_input(L0_ffn_gate_w), by_input(L0_ffn_up_w)], axis=1)),
        "w_down": rows(np.concatenate([by_feature(L0_ffn_down_w), by_feature(L0_ffn_lora_B)], axis=0)),
    }
    arrays.update(constants())
    nc = _bacc.Bacc("TRN2", target_bir_lowering=False, num_devices=1)
    aps = {n: nc.dram_tensor(n, a.shape, mybir.dt.from_np(a.dtype), kind="ExternalInput").ap()
           for n, a in arrays.items()}
    aps["out"] = nc.dram_tensor("out", (SEQ, DM), mybir.dt.float32, kind="ExternalOutput").ap()
    decoder_layer(nc, **aps)
    r = _run(nc, [arrays], core_ids=[0])
    return r.results[0]["out"].reshape(1, SEQ, DM)
```

```python
import numpy as np
import concourse.bass as bass
from concourse import mybir
from contextlib import ExitStack


SEQ, DM, HEADS, HD = 2048, 256, 16, 16
TOK = 128
TILE = 512
TILES = SEQ // TILE
SUBS = TILE // TOK
HPI = HEADS // SUBS
CH = DM // 128
EXPERTS, FF, RANK = 8, 32, 16
GU = 2 * EXPERTS * FF
LORA = EXPERTS * RANK
LR = LORA + EXPERTS
DOWN = (EXPERTS * FF + LORA) // 128
EPS = 1e-5

PARTS = 3
PAIRS = [(0, 0), (0, 1), (1, 0), (0, 2), (2, 0), (1, 1)]
ROW_QK = 4 * PARTS
ROW_SHIFT = ROW_QK + len(PAIRS) * HD
ROW_END = ROW_SHIFT + PARTS
VC = PARTS * HD + 1
MASKED = -1e30

CHUNK = TILE
RING = [12, 14, 11, 12]
SCAN_BANKS = 3
SCORE_BANKS = [2, 2, 2, 2 + SCAN_BANKS]
PBUF = 4
LAG = 8
SPLIT_LAG = 3
SPLIT_ON_VECTOR = [set(), set(), {5}, {0, 1, 3, 4, 6, 7, 9, 10, 12, 13}]
START = 16
SCALE = 1.0 / HD ** 0.5


def chunks_of(t):
    return SUBS * t + SUBS - 1


def chunk_blocks(t, j):
    k = SUBS * t
    if j <= k:
        return [(j, 0, 0, TILE)]
    if j == k + 1:
        return [(k + 1, 1, 0, 3 * TOK), (k + 3, 3, 3 * TOK, TOK)]
    return [(k + 2, 2, 0, 2 * TOK)]


def chunk_width(t, j):
    return 2 * TOK if j == chunks_of(t) - 1 else TILE


def bank_user(i, banks, before):
    return i - banks if i >= banks else -1 - (before - 1 - i) % banks


def ring_user(i, t, first):
    assert HPI * chunks_of(t) % RING[t] == 0
    if i >= RING[t] or not first or t == 0:
        return i - RING[t]
    return i - RING[t - 1] if i < RING[t - 1] else -HPI * chunks_of(t - 1)


def chunks_before(t):
    return HEADS * sum(chunks_of(i) for i in range(t))


def maxes_before(t):
    return HEADS * SUBS * sum(i + 1 for i in range(t))


def splits_before(t, j, vector):
    return sum((i in SPLIT_ON_VECTOR[t]) == vector for i in range(j))


def all_splits_before(t, vector):
    return HEADS * sum(splits_before(i, chunks_of(i), vector) for i in range(t))


FFN_STEPS = ["y", "yT", "yT out", "proj", "x1", "rstd", "", "norm", "hT", "hT out", "route", "route max",
             "route exp", "select", "", "gate", "tanh", "gated", "", "gT", "gT out", "down", "out"]


def turn(attend, scan, feed, late, shifted):
    n = HPI * chunks_of(attend) if attend is not None else 0
    slots = n or 12
    scans = HPI * SUBS * (scan + 1) if scan is not None else 0
    first = 0 if attend is None else LAG + 1 if late == feed else SHIFT_SLOT + 1
    steps, done, fed = [("shift parts", 0, 1)] if shifted else [], 0, 0
    for i in range(slots):
        if i < n:
            steps.append(("scores", i, 0))
        if SPLIT_LAG <= i < n:
            steps.append(("split", i - SPLIT_LAG, 0))
        if shifted and i in (SHIFT_SLOT, SHIFT_SLOT + 1):
            steps.append((("shift", "shift out")[i - SHIFT_SLOT], 0, 1))
        pieces = []
        if i < LAG and late is not None:
            m = HPI * chunks_of(late) - LAG + i
            pieces = [("mix high", m, 1), ("mix low", m, 1)]
        elif n and i >= LAG:
            pieces = [("mix high", i - LAG, 0), ("mix low", i - LAG, 0)]
        while done * slots < scans * (i + 1) and done < scans:
            steps.append(("scan", done, 0))
            done += 1
            if pieces:
                steps.append(pieces.pop(0))
        steps += pieces
        while (feed is not None and i >= first and fed < len(FFN_STEPS)
               and fed * (slots - first) < len(FFN_STEPS) * (i - first + 1)):
            steps.append((FFN_STEPS[fed], 0, 0))
            fed += 1
    if n:
        steps += [("split", n - SPLIT_LAG + k, 0) for k in range(SPLIT_LAG)]
    assert feed is None or fed == len(FFN_STEPS)
    return steps


def drain(late):
    n = HPI * chunks_of(late)
    return [(name, n - LAG + i, 1) for i in range(LAG) for name in ("mix high", "mix low")]


def side_by_side():
    order = sorted((k + SKEW * q, q, name) for k, name in enumerate(FFN_STEPS) for q in range(SUBS) if name)
    return [(name, q, 0) for _, q, name in order]


STAGES = ([(None, 0, None)]
          + [(t, t + 1 if t + 1 < TILES else None, t - 1 if t else None) for t in range(TILES)]
          + [(None, None, TILES - 1)])


def run_stages(engine, body):
    for attend, scan, feed in STAGES:
        tiles = (attend, scan, feed)
        if attend is None and feed is not None:
            body(0, drain(feed), (None, None, None), (feed, SUBS - 1, 0), None)
            body(None, side_by_side(), tiles, None, None)
            continue
        before = attend - 1 if attend else None
        shifted = (attend, SUBS - 1, 0) if attend is not None else None
        body(0, turn(attend, scan, feed, before, bool(shifted)), tiles, (before, SUBS - 1, 0), shifted)
        shifted = scan is not None
        with engine.Fori(1, SUBS) as u:
            body(u, turn(attend, scan, feed, attend, shifted), tiles, (attend, u, 1),
                 (scan, u, 1) if shifted else None)


SHIFT_SLOT = 2
SKEW = 1
FFN_LINKS = 11
SHIFT_LINKS = 5


class Workspace:

    def __init__(self, bank, xd, yn, tT, g, gT, res, e16, left, top8, top2, rsm, wexp, stats, mv, ve, rstd):
        self.bank, self.xd, self.yn, self.tT, self.g, self.gT, self.res = bank, xd, yn, tT, g, gT, res
        self.e16, self.left, self.top8, self.top2, self.rsm, self.wexp = e16, left, top8, top2, rsm, wexp
        self.stats, self.mv, self.ve, self.rstd = stats, mv, ve, rstd
        self.rden = g[:, 0:HEADS]


def decoder_layer(nc, x, c_cols, wmod, wqkv, wo, w_lr, w_gu, w_down, alibi_k, alibi_q, ident,
                  mask_q, mask_k, out):
    f32, bf16, f16 = mybir.dt.float32, mybir.dt.bfloat16, mybir.dt.float16
    ALU, ACT, AX = mybir.AluOpType, mybir.ActivationFunctionType, mybir.AxisListType

    x_t = x.rearrange("(t s p) d -> t p s d", s=SUBS, p=TOK)
    out_t = out.rearrange("(t s p) d -> t p s d", s=SUBS, p=TOK)
    scratch = nc.dram_tensor("qk_parts", [2, PARTS, DM, SEQ], bf16, kind="Internal").ap()

    ctx = ExitStack()
    with ctx:
        def sb(name, shape, dt):
            return ctx.enter_context(nc.sbuf_tensor(name, shape, dt))

        def sem(name):
            return ctx.enter_context(nc.semaphore(name))

        loop_sems = []

        def loop_sem(name):
            loop_sems.append(sem(name))
            return loop_sems[-1]

        ka = sb("ka", [128, HEADS, SEQ], bf16)
        qa = sb("qa", [128, 2, HEADS, TILE], bf16)
        vp = sb("vp", [128, SEQ // TOK, HEADS, VC], bf16)
        probs = sb("probs", [128, max(RING), CHUNK], f32)
        probs_lo = sb("probs_lo", [128, max(RING), CHUNK], f16)
        yraw = sb("yraw", [128, 2, SUBS, HEADS, VC], f32)
        wo_sb = sb("wo_sb", [128, CH, DM], f32)
        w_lr_sb = sb("w_lr_sb", [128, CH, LR], f32)
        w_gu_sb = sb("w_gu_sb", [128, CH, GU], f32)
        w_down_sb = sb("w_down_sb", [128, DOWN, DM], f32)
        idf = sb("idf", [128, 128], f32)
        idb = sb("idb", [128, 128], bf16)
        mask_q_sb = sb("mask_q_sb", [128, 128], bf16)
        mask_k_sb = sb("mask_k_sb", [128, 128], bf16)
        xd = sb("xd", [128, DM], f32)
        yn = sb("yn", [128, DM], f32)
        tT = sb("tT", [128, CH, TOK], f32)
        g = sb("g", [128, EXPERTS * FF + LORA], f32)
        gT = sb("gT", [128, DOWN, TOK], f32)
        res = sb("res", [128, DM], f32)
        stats = sb("stats", [128, SUBS, 6], f32)
        mv = sb("mv", [128, SUBS, 2], f32)
        ve = sb("ve", [128, SUBS], f32)
        rstd = sb("rstd", [128, SUBS], f32)
        minus_half = sb("minus_half", [128, SUBS], f32)
        modc = sb("modc", [128, 4, CH], f32)
        silc = sb("silc", [128, 4, CH], f32)
        e16 = sb("e16", [128, SUBS, 2 * EXPERTS], f32)
        left = sb("left", [128, SUBS, 2 * EXPERTS], f32)
        top8 = sb("top8", [128, SUBS, 8], f32)
        top2 = sb("top2", [128, SUBS, 8], f32)
        rsm = sb("rsm", [128, SUBS, 3], f32)
        wexp = sb("wexp", [128, SUBS, 3, EXPERTS], f32)
        part_max = sb("part_max", [128, HPI * SUBS, TILES], f32)
        neg_max = sb("neg_max", [128, 3, HPI * SUBS], f32)
        shift = sb("shift", [128, 128], bf16)
        shift_rows = sb("shift_rows", [PARTS * HPI * SUBS, TOK], bf16)

        ring = probs[:, :, :].rearrange("p a b -> p (a b)")
        wqkv_sb = ring[:, 0:1536].rearrange("p (c e) -> p c e", c=CH)
        xin = ring[:, 1536:3584].rearrange("p (b s d) -> p b s d", b=2, s=SUBS)
        hT = ring[:, 3584:5632].rearrange("p (b c t) -> p b c t", b=2, c=CH)
        nrm = ring[:, 5632:6656].rearrange("p (b d) -> p b d", b=SUBS)
        low = probs_lo[:, :, :].rearrange("p a b -> p (a b)")
        parts = low[:, 0:6144].bitcast(bf16).rearrange("p (b a t) -> p b a t", b=PBUF, a=PARTS)
        resid = [ring[:, 6656:7168], low[:, 6144:7168].bitcast(f32)]
        raw = yraw[:, :, :, :, :].rearrange("p a b c d -> p (a b c d)")
        wmod_sb = raw[:, 0:3072].rearrange("p (c e) -> p c e", c=CH)
        silb = raw[:, 3072:3328].rearrange("p (c t) -> p c t", c=CH)
        gates = raw[:, 3328:4352].rearrange("p (a e) -> p a e", a=2)
        resid_v = raw[:, 4352:5376].rearrange("p (b t) -> p b t", b=2)

        bank = ctx.enter_context(nc.psum_tensor("bank", [128, 8, 512], f32))
        SCAN, MIX, MISC = 2, 5, 7

        def workspace(q):
            big = [("xd", DM), ("yn", DM), ("tT", CH * TOK), ("g", EXPERTS * FF + LORA), ("gT", DOWN * TOK),
                   ("res", DM)]
            if q == 0:
                w = {"xd": xd[:, :], "yn": yn[:, :], "tT": tT[:, :, :], "g": g[:, :], "gT": gT[:, :, :],
                     "res": res[:, :]}
            else:
                w, a = {}, (q - 1) * sum(n for _, n in big)
                for name, n in big:
                    w[name] = ring[:, a:a + n]
                    a += n
                w["tT"] = w["tT"].rearrange("p (c t) -> p c t", c=CH)
                w["gT"] = w["gT"].rearrange("p (c t) -> p c t", c=DOWN)
            return Workspace(
                bank=bank[:, MISC if q == 0 else q - 1, :], e16=e16[:, q, :], left=left[:, q, :],
                top8=top8[:, q, :], top2=top2[:, q, :], rsm=rsm[:, q, :], wexp=wexp[:, q, :, :],
                stats=stats[:, q, :], mv=mv[:, q, :], ve=ve[:, q:q + 1], rstd=rstd[:, q:q + 1], **w)

        work = [workspace(q) for q in range(SUBS)]

        c_in = sem("c_in")
        w_mod = [sem("w_mod0"), sem("w_mod1")]
        w_in = sem("w_in")
        w_rest = sem("w_rest")
        consts = sem("consts")
        masks = sem("masks")
        made = sem("made")
        fill = sem("fill")
        x_in = [sem(f"x_in{b}") for b in range(2)]
        own = sem("own")
        sil_th = sem("sil_th")
        sil_ready = sem("sil_ready")
        mod_psum = sem("mod_psum")
        mod_ready = sem("mod_ready")
        var1 = sem("var1")
        rstd1 = sem("rstd1")
        n1 = sem("n1")
        hT_psum = sem("hT_psum")
        hT_ready = sem("hT_ready")
        qk_psum = sem("qk_psum")
        qk_hi = sem("qk_hi")
        qk_mid = sem("qk_mid")
        qk_lo = sem("qk_lo")
        v_psum = sem("v_psum")
        v_hi = sem("v_hi")
        v_mid = sem("v_mid")
        v_lo = sem("v_lo")
        stored = [sem(f"stored{b}") for b in range(PBUF)]
        k_rows = [sem(f"k_rows{t}") for t in range(TILES)]
        q_rows = [sem("q_rows0"), sem("q_rows1"), loop_sem("q_rows2"), loop_sem("q_rows3")]
        scan_psum = loop_sem("scan_psum")
        scan_max = loop_sem("scan_max")
        shift_own = loop_sem("shift_own")
        shift_psum = loop_sem("shift_psum")
        shift_sb = loop_sem("shift_sb")
        shift_in = loop_sem("shift_in")
        scores_psum = loop_sem("scores_psum")
        exp_done = loop_sem("exp_done")
        split_v = loop_sem("split_v")
        split_g = loop_sem("split_g")
        mixed = loop_sem("mixed")
        y_out = loop_sem("y_out")
        xd_in = loop_sem("xd_in")
        ffn_own = loop_sem("ffn_own")
        y_ready = loop_sem("y_ready")
        yT_psum = loop_sem("yT_psum")
        yT_ready = loop_sem("yT_ready")
        proj_psum = loop_sem("proj_psum")
        x1_var = loop_sem("x1_var")
        rstd2 = loop_sem("rstd2")
        n2 = loop_sem("n2")
        n2T_psum = loop_sem("n2T_psum")
        h2T_ready = loop_sem("h2T_ready")
        route_psum = loop_sem("route_psum")
        route_max = loop_sem("route_max")
        route_exp = loop_sem("route_exp")
        lora_done = loop_sem("lora_done")
        gu_psum = loop_sem("gu_psum")
        tanh_done = loop_sem("tanh_done")
        gated = loop_sem("gated")
        gT_psum = loop_sem("gT_psum")
        gT_ready = loop_sem("gT_ready")
        down_psum = loop_sem("down_psum")
        res_ready = loop_sem("res_ready")
        res_out = loop_sem("res_out")
        unread = sem("unread")

        def wait_alone(engine, semaphore, value):
            engine.wait_ge(semaphore, value)
            engine.sem_inc(unread, 1)

        def pair(a):
            return a.rearrange("p (s h d) -> p s h d", s=2, d=HD)

        def v_part(n, a):
            return vp[:, 2 * n:2 * n + 2, :, HD * a:HD * (a + 1)]

        def at(base, per_turn, u, k, back=0):
            return u * per_turn + (base + k - back * per_turn + START)

        def chunk_at(semaphore_tile, u, k, back=0):
            return at(chunks_before(semaphore_tile), HPI * chunks_of(semaphore_tile), u, k, back)

        def place_free(i, t, u):
            return chunk_at(t, u, ring_user(i, t, isinstance(u, int)) + 1)

        def bank_free(i, t, u):
            if isinstance(u, int) and t and i < SCORE_BANKS[t]:
                before = HPI * chunks_of(t - 1)
                i = min(i, SCORE_BANKS[t - 1] - 1)
                return chunk_at(t, u, bank_user(i, SCORE_BANKS[t - 1], before) + 1)
            return chunk_at(t, u, bank_user(i, SCORE_BANKS[t], HPI * chunks_of(t)) + 1)

        def scan_bank_free(i, t, u):
            before = t - 1 if t and isinstance(u, int) else t
            return at(maxes_before(t), HPI * SUBS * (t + 1), u,
                      bank_user(i, SCAN_BANKS, HPI * SUBS * (before + 1)) + 1)

        def link_at(feed, u, k):
            if u is None:
                return at(FFN_LINKS * SUBS * feed, 0, 0, k)
            return at(FFN_LINKS * SUBS * feed, FFN_LINKS, u, k)

        def mix_place(i, back, tiles, u, past):
            t, at_u, back = past if back else (tiles[0], u, 0)
            return t, at_u, back, i // chunks_of(t), i % chunks_of(t)

        block = ctx.enter_context(nc.Block())

        @block.sync
        def _(sp):
            sp.dma_start(silc[:, 0, :], c_cols).then_inc(c_in, 16)
            sp.dma_start(xin[:, 0, :, :], x_t[0]).then_inc(x_in[0], 16)
            sp.dma_start(idf[:, :], ident).then_inc(consts, 16)
            sp.dma_start(wmod_sb[:, :, 0:2 * DM], wmod[:, :, 0:2 * DM]).then_inc(w_mod[0], 16)
            sp.dma_start(wqkv_sb, wqkv).then_inc(w_in, 16)
            sp.dma_start(xin[:, 1, :, :], x_t[1]).then_inc(x_in[1], 16)
            sp.dma_start(wmod_sb[:, :, 2 * DM:], wmod[:, :, 2 * DM:]).then_inc(w_mod[1], 16)
            sp.dma_start(mask_q_sb[:, :], mask_q).then_inc(masks, 16)
            sp.dma_start(mask_k_sb[:, :], mask_k).then_inc(masks, 16)
            sp.dma_start(ka[0:ROW_QK, :, :], alibi_k[0:ROW_QK]).then_inc(fill, 16)
            sp.dma_start(ka[ROW_SHIFT:ROW_END, :, :], alibi_k[ROW_QK:ROW_QK + PARTS]).then_inc(fill, 16)
            sp.dma_start(wo_sb[:, :, :], wo).then_inc(w_rest, 16)
            sp.dma_start(w_down_sb[:, :, :], w_down).then_inc(w_rest, 16)
            sp.dma_start(w_lr_sb[:, :, :], w_lr).then_inc(w_rest, 16)
            sp.dma_start(w_gu_sb[:, :, :], w_gu).then_inc(w_rest, 16)
            for t in range(TILES):
                for j in range(2 * CH):
                    n = 2 * CH * t + j
                    sp.wait_ge(qk_lo, n + 1)
                    sp.dma_start(
                        scratch[j // CH, :, 128 * (j % CH):128 * (j % CH + 1), TILE * t:TILE * (t + 1)]
                        .rearrange("a p t -> p a t"), parts[:, n % PBUF, :, :]).then_inc(stored[n % PBUF], 16)
                if t + 2 < TILES:
                    sp.wait_ge(n1, SUBS * (t + 1))
                    sp.dma_start(xin[:, t % 2, :, :], x_t[t + 2]).then_inc(x_in[t % 2], 16)
                for b in range(PBUF):
                    sp.wait_ge(stored[b], 16 * (2 * CH // PBUF) * (t + 1))
                for i, (pq, pk) in enumerate(PAIRS):
                    rows = slice(ROW_QK + HD * i, ROW_QK + HD * (i + 1))
                    sp.dma_start(ka[rows, :, TILE * t:TILE * (t + 1)],
                                 scratch[1, pk, :, TILE * t:TILE * (t + 1)]
                                 .rearrange("(h d) t -> d h t", d=HD)).then_inc(k_rows[t], 16)
                    if t < 2:
                        sp.dma_start(qa[rows, t, :, :],
                                     scratch[0, pq, :, TILE * t:TILE * (t + 1)]
                                     .rearrange("(h d) t -> d h t", d=HD)).then_inc(q_rows[t], 16)
                if t < 2:
                    sp.dma_start(qa[0:ROW_QK, t, :, :],
                                 alibi_q[:, :, TILE * t:TILE * (t + 1)]).then_inc(q_rows[t], 16)

            def body(u, steps, tiles, past, shifted):
                attend, scan, feed = tiles
                if u is None:
                    sp.wait_ge(res_ready, at(SUBS * feed, 0, 0, 0))
                    sp.wait_ge(y_out, at(HEADS * TILES, 0, 0, 0))
                    for q in range(SUBS):
                        sp.dma_start(work[q].xd, x_t[feed, :, q, :]).then_inc(xd_in, 16)
                    for q in range(SUBS):
                        sp.wait_ge(res_ready, at(SUBS * feed + q, 0, 0, 1))
                        sp.dma_start(out_t[feed, :, q, :], work[q].res).then_inc(res_out, 16)
                    return
                if feed is not None:
                    wait_alone(sp, res_ready, at(SUBS * feed, 1, u, 0))
                    sp.dma_start(xd[:, :], x[bass.ds(u * TOK + feed * TILE, TOK), :]).then_inc(xd_in, 16)
                if shifted is not None:
                    t, at_u, ago = shifted
                    wait_alone(sp, shift_sb, at(SUBS * t, 1, at_u, 1, ago))
                    for p in range(PARTS):
                        sp.dma_start(
                            qa[ROW_SHIFT + p:ROW_SHIFT + p + 1, t % 2,
                               bass.ds(at_u * HPI - ago * HPI, HPI), :],
                            shift_rows[HPI * SUBS * p:HPI * SUBS * (p + 1), :]).then_inc(shift_in, 16)
                    wait_alone(sp, shift_in, at(16 * PARTS * SUBS * t, 16 * PARTS, at_u, 16 * PARTS, ago))
                if feed is not None:
                    wait_alone(sp, res_ready, at(SUBS * feed, 1, u, 1))
                    sp.dma_start(out[bass.ds(u * TOK + feed * TILE, TOK), :], res[:, :]).then_inc(res_out, 16)
                    wait_alone(sp, res_out, at(16 * SUBS * feed, 16, u, 16))
                if attend is not None and attend + 2 < TILES:
                    t = attend + 2
                    wait_alone(sp, scores_psum, chunk_at(attend, u, HPI * chunks_of(attend)))
                    wait_alone(sp, q_rows[t], at(0, 16 * (len(PAIRS) + 1), u, 0))
                    for i, (pq, _) in enumerate(PAIRS):
                        sp.dma_start(qa[ROW_QK + HD * i:ROW_QK + HD * (i + 1), t % 2, bass.ds(u * HPI, HPI), :],
                                     scratch[0, pq, bass.ds(u * HPI * HD, HPI * HD), TILE * t:TILE * (t + 1)]
                                     .rearrange("(h d) t -> d h t", d=HD)).then_inc(q_rows[t], 16)
                    sp.dma_start(qa[0:ROW_QK, t % 2, bass.ds(u * HPI, HPI), :],
                                 alibi_q[:, bass.ds(u * HPI, HPI), TILE * t:TILE * (t + 1)])\
                        .then_inc(q_rows[t], 16)

            run_stages(sp, body)
            sp.wait_ge(res_out, at(16 * SUBS * TILES, 0, 0, 0))

        @block.gpsimd
        def _(pool):
            for s in loop_sems:
                pool.sem_inc(s, START)
            pool.memset(minus_half[:, :], -0.5).then_inc(made, 1)
            pool.memset(e16[:, :, :], -1.0).then_inc(made, 1)
            pool.memset(top2[:, :, :], -1.0).then_inc(made, 1)
            pool.memset(shift[:, :], 0.0).then_inc(made, 1)
            pool.memset(vp[:, :, :, VC - 1:VC], 1.0).then_inc(made, 1)
            def inverse_std(t):
                pool.wait_ge(var1, t + 1)
                pool.tensor_tensor(rstd[:, :], ve[:, :], minus_half[:, :], ALU.pow).then_inc(rstd1, 1)

            pool.wait_ge(made, 5)
            inverse_std(0)
            for t in range(TILES):
                if t + 1 < TILES:
                    inverse_std(t + 1)
                for j in range(2 * CH):
                    n = 2 * CH * t + j
                    pool.wait_ge(qk_mid, n + 1)
                    pool.tensor_tensor(parts[:, n % PBUF, 2, :], resid[j % 2], parts[:, n % PBUF, 1, :],
                                       ALU.subtract).then_inc(qk_lo, 1)
                for b in range(2):
                    n = 2 * t + b
                    pool.wait_ge(v_mid, n + 1)
                    pool.tensor_tensor(v_part(n, 2), pair(resid_v[:, b, :]), v_part(n, 1),
                                       ALU.subtract).then_inc(v_lo, 1)

            def body(u, steps, tiles, past, shifted):
                attend, scan, feed = tiles
                for step, i, back in steps:
                    ws, place = (work[0], u) if u is not None else (work[i], i)
                    if step == "split":
                        t, nc_ = attend, chunks_of(attend)
                        hh, j = i // nc_, i % nc_
                        if j in SPLIT_ON_VECTOR[t]:
                            continue
                        w = chunk_width(t, j)
                        pool.wait_ge(exp_done, chunk_at(t, u, i + 1))
                        pool.wait_ge(mixed, place_free(i, t, u))
                        p = probs[:, i % RING[t], 0:w]
                        pool.tensor_tensor(probs_lo[:, i % RING[t], 0:w], p, p.bitcast(bf16)[:, 1::2],
                                           ALU.subtract).then_inc(split_g, 1)
                    elif step == "rstd":
                        pool.wait_ge(x1_var, at(SUBS * feed, 1, place, 1))
                        pool.tensor_tensor(ws.rstd, ws.ve, minus_half[:, 0:1],
                                           ALU.pow).then_inc(rstd2, 1)

            run_stages(pool, body)

        @block.scalar
        def _(act):
            act.wait_ge(c_in, 16)
            act.activation(silc[:, 1, :], silc[:, 0, :], ACT.Tanh, scale=0.5).then_inc(sil_th, 1)

            def modulate(t):
                act.wait_ge(hT_psum, SUBS * (t + 1))
                if t == 0:
                    act.wait_ge(mod_ready, 1)
                if t >= 2:
                    act.wait_ge(v_psum, 2 * (t - 1))
                for c in range(CH):
                    act.activation(hT[:, t % 2, c, :], bank[:, c, :], ACT.Identity,
                                   scale=modc[:, 0, c:c + 1], bias=modc[:, 1, c:c + 1]).then_inc(hT_ready, 1)

            modulate(0)
            for t in range(TILES):
                for j in range(2 * CH):
                    n = 2 * CH * t + j
                    act.wait_ge(qk_psum, n + 1)
                    if n >= PBUF:
                        act.wait_ge(stored[n % PBUF], 16 * (n // PBUF))
                    act.activation(parts[:, n % PBUF, 0, :], bank[:, 2 + j, :], ACT.Copy).then_inc(qk_hi, 1)
                if t + 1 < TILES:
                    modulate(t + 1)
                for b in range(2):
                    n = 2 * t + b
                    act.wait_ge(v_psum, n + 1)
                    act.activation(v_part(n, 0), pair(bank[:, 6 + b, :]), ACT.Copy).then_inc(v_hi, 1)
            act.wait_ge(v_lo, 2 * TILES)
            act.wait_ge(mod_ready, 4)

            def body(u, steps, tiles, past, shifted):
                attend, scan, feed = tiles
                for step, i, back in steps:
                    ws, place = (work[0], u) if u is not None else (work[i], i)
                    if step == "scores":
                        t, nc_ = attend, chunks_of(attend)
                        w = chunk_width(t, i % nc_)
                        act.wait_ge(mixed, place_free(i, t, u))
                        act.wait_ge(scores_psum, chunk_at(t, u, i + 1))
                        act.activation(probs[:, i % RING[t], 0:w], bank[:, i % SCORE_BANKS[t], 0:w], ACT.Exp,
                                       scale=SCALE).then_inc(exp_done, 1)
                    elif step == "mix low":
                        t, at_u, ago, hh, j = mix_place(i, back, tiles, u, past)
                        if j == chunks_of(t) - 1:
                            act.wait_ge(mixed, chunk_at(t, at_u, i + 1, ago))
                            act.activation(yraw[:, t % 2, :, at_u * HPI + (hh - ago * HPI), :],
                                           bank[:, MIX + hh % 2, 0:SUBS * VC].rearrange("p (s v) -> p s v", v=VC),
                                           ACT.Copy).then_inc(y_out, 1)
                    elif step == "yT out":
                        act.wait_ge(yT_psum, at(SUBS * feed, 1, place, 1))
                        act.activation(ws.tT.rearrange("p c t -> p (c t)"), ws.bank[:, 0:DM],
                                       ACT.Copy).then_inc(yT_ready, 1)
                    elif step == "hT out":
                        act.wait_ge(n2T_psum, at(SUBS * feed, 1, place, 1))
                        for c in range(CH):
                            act.activation(ws.tT[:, c, :], ws.bank[:, TOK * c:TOK * (c + 1)], ACT.Identity,
                                           scale=modc[:, 2, c:c + 1], bias=modc[:, 3, c:c + 1])\
                                .then_inc(h2T_ready, 1)
                    elif step == "route exp":
                        act.wait_ge(route_max, at(SUBS * feed, 1, place, 1))
                        act.activation(ws.e16[:, 0:EXPERTS], ws.bank[:, LORA:LR], ACT.Exp,
                                       bias=ws.rsm[:, 0:1], accum_out=ws.rsm[:, 1:2]).then_inc(route_exp, 1)
                    elif step == "tanh":
                        act.wait_ge(gu_psum, at(SUBS * feed, 1, place, 1))
                        act.activation(ws.g[:, 0:EXPERTS * FF], ws.bank[:, 0:EXPERTS * FF], ACT.Tanh,
                                       scale=0.5).then_inc(tanh_done, 1)
                    elif step == "gT out":
                        act.wait_ge(gT_psum, at(SUBS * feed, 1, place, 1))
                        act.activation(ws.gT.rearrange("p c t -> p (c t)"),
                                       ws.bank[:, 0:DOWN * TOK], ACT.Copy).then_inc(gT_ready, 1)
                    elif step == "shift out":
                        t, at_u, ago = shifted
                        act.wait_ge(shift_psum, at(SUBS * t, 1, at_u, 1, ago))
                        act.wait_ge(shift_in, at(16 * PARTS * SUBS * t, 16 * PARTS, at_u, 0, ago))
                        act.activation(shift_rows[:, :],
                                       bank[0:PARTS * HPI * SUBS, MISC, 0:TOK // 2].bitcast(bf16),
                                       ACT.Copy).then_inc(shift_sb, 1)

            run_stages(act, body)

        @block.vector
        def _(dve):
            links = [0]

            def link(ins):
                links[0] += 1
                ins.then_inc(own, 1)
                dve.wait_ge(own, links[0])

            def norm_tile(t):
                dve.wait_ge(x_in[t % 2], 16 * (t // 2 + 1))
                for s in range(SUBS):
                    ins = dve.bn_stats(stats[:, s, :], xin[:, t % 2, s, :])
                link(ins)
                for s in range(SUBS):
                    ins = dve.bn_aggr(mv[:, s, :], stats[:, s, :])
                link(ins)
                dve.tensor_scalar(ve[:, :], mv[:, :, 1], EPS, None, ALU.add).then_inc(var1, 1)
                dve.wait_ge(rstd1, t + 1)
                for s in range(SUBS):
                    if t:
                        dve.wait_ge(hT_psum, SUBS * t)
                    dve.tensor_scalar(nrm[:, s, :], xin[:, t % 2, s, :], mv[:, s, 0:1], rstd[:, s:s + 1],
                                      ALU.subtract, ALU.mult).then_inc(n1, 1)

            dve.wait_ge(sil_th, 1)
            link(dve.scalar_tensor_tensor(out=silc[:, 2, :], in0=silc[:, 1, :], scalar=1.0, in1=silc[:, 0, :],
                                          op0=ALU.add, op1=ALU.mult))
            dve.tensor_scalar(silc[:, 3, :], silc[:, 2, :], 0.5, None, ALU.mult).then_inc(sil_ready, 1)
            norm_tile(0)
            link(dve.memset(silb, 1.0))
            dve.wait_ge(sil_ready, 1)
            for c in range(CH):
                ins = dve.tensor_scalar(silb[:, c, :], silb[:, c, :], silc[:, 3, c:c + 1], None, ALU.mult)
            ins.then_inc(sil_ready, 1)

            def columns(m):
                dve.wait_ge(mod_psum, m + 1)
                cols = bank[:, 7 if m == 0 else 1, 0:2 * CH].rearrange("p (v c) -> p v c", c=CH)
                dve.tensor_copy(modc[:, 2 * m + 1, :], cols[:, 0, :])
                dve.tensor_scalar(modc[:, 2 * m, :], cols[:, 1, :], 1.0, None, ALU.add).then_inc(mod_ready, 1)

            def scale_by_gates():
                g_psum = bank[:, 0, :]
                link(dve.tensor_scalar(gates[:, 0, :], g_psum, 0.0, 2.0, ALU.is_ge, ALU.mult))
                dve.scalar_tensor_tensor(out=gates[:, 1, :], in0=gates[:, 0, :], scalar=-1.0,
                                         in1=g_psum, op0=ALU.add, op1=ALU.mult).then_inc(mod_ready, 1)
                dve.wait_ge(mod_ready, 3)
                link(dve.tensor_scalar(gates[:, 1, :], gates[:, 1, :], 0.25, None, ALU.max))
                link(dve.scalar_tensor_tensor(out=gates[:, 0, :], in0=gates[:, 0, :], scalar=-1.0,
                                              in1=gates[:, 1, :], op0=ALU.add, op1=ALU.mult))
                dve.wait_ge(w_rest, 64)
                for w_sb, n, a in ((wo_sb, CH, 0), (w_down_sb, DOWN, DM)):
                    for c in range(n):
                        ins = dve.tensor_tensor(w_sb[:, c, :], w_sb[:, c, :], gates[:, 0, a:a + DM], ALU.mult)
                ins.then_inc(mod_ready, 1)
                dve.wait_ge(consts, 16)
                dve.tensor_copy(idb[:, :], idf[:, :]).then_inc(mod_ready, 1)

            columns(0)
            for t in range(TILES):
                if t + 1 < TILES:
                    norm_tile(t + 1)
                for j in range(2 * CH):
                    n = 2 * CH * t + j
                    dve.wait_ge(qk_hi, n + 1)
                    if n >= 2:
                        dve.wait_ge(qk_lo, n - 1)
                    link(dve.tensor_tensor(resid[j % 2], bank[:, 2 + j, :], parts[:, n % PBUF, 0, :],
                                           ALU.subtract))
                    dve.tensor_copy(parts[:, n % PBUF, 1, :], resid[j % 2]).then_inc(qk_mid, 1)
                for b in range(2):
                    n = 2 * t + b
                    dve.wait_ge(v_hi, n + 1)
                    if n >= 2:
                        dve.wait_ge(v_lo, n - 1)
                    r = pair(resid_v[:, b, :])
                    link(dve.tensor_tensor(r, pair(bank[:, 6 + b, :]), v_part(n, 0), ALU.subtract))
                    dve.tensor_copy(v_part(n, 1), r).then_inc(v_mid, 1)
                if t == 0:
                    columns(1)
                    scale_by_gates()
            dve.wait_ge(made, 5)

            def body(u, steps, tiles, past, shifted):
                attend, scan, feed = tiles
                k = [0]

                def ffn_link(ins, wait=dve.wait_ge):
                    k[0] += 1
                    ins.then_inc(ffn_own, 1)
                    wait(ffn_own, link_at(feed, u, k[0]))

                def alone(semaphore, value):
                    wait_alone(dve, semaphore, value)

                for step, i, back in steps:
                    ws, place = (work[0], u) if u is not None else (work[i], i)
                    if step == "scan":
                        r, c = (i // (scan + 1)), i % (scan + 1)
                        w = TILE if c < scan else TOK * (r % SUBS + 1)
                        dve.wait_ge(scan_psum, at(maxes_before(scan), HPI * SUBS * (scan + 1), u, i + 1))
                        dve.tensor_reduce(part_max[:, r, c:c + 1], bank[:, SCAN + i % SCAN_BANKS, 0:w], AX.X,
                                          ALU.max).then_inc(scan_max, 1)
                    elif step == "shift parts":
                        t, at_u, ago = shifted
                        kk = [0]

                        def shift_link(ins):
                            kk[0] += 1
                            ins.then_inc(shift_own, 1)
                            dve.wait_ge(shift_own, at(SHIFT_LINKS * SUBS * t, SHIFT_LINKS, at_u, kk[0], ago))

                        per = HPI * SUBS * (t + 1)
                        dve.wait_ge(scan_max, at(maxes_before(t), per, at_u, per, ago))
                        shift_link(dve.tensor_reduce(neg_max[:, 0, :], part_max[:, :, 0:t + 1], AX.X,
                                                     ALU.max, negate=True))
                        n = HPI * SUBS
                        dve.wait_ge(shift_psum, at(SUBS * t, 1, at_u, 0, ago))
                        shift_link(dve.tensor_copy(shift[:, 0:n], neg_max[:, 0, :]))
                        shift_link(dve.tensor_tensor(neg_max[:, 1, :], neg_max[:, 0, :], shift[:, 0:n],
                                                     ALU.subtract))
                        shift_link(dve.tensor_copy(shift[:, n:2 * n], neg_max[:, 1, :]))
                        shift_link(dve.tensor_tensor(shift[:, 2 * n:3 * n], neg_max[:, 1, :],
                                                     shift[:, n:2 * n], ALU.subtract))
                        assert kk[0] == SHIFT_LINKS
                    elif step == "split":
                        t, nc_ = attend, chunks_of(attend)
                        j = i % nc_
                        if j not in SPLIT_ON_VECTOR[t]:
                            continue
                        w = chunk_width(t, j)
                        dve.wait_ge(exp_done, chunk_at(t, u, i + 1))
                        dve.wait_ge(mixed, place_free(i, t, u))
                        p = probs[:, i % RING[t], 0:w]
                        dve.tensor_tensor(probs_lo[:, i % RING[t], 0:w], p, p.bitcast(bf16)[:, 1::2],
                                          ALU.subtract).then_inc(split_v, 1)
                    elif step == "y":
                        dve.wait_ge(y_out, at(HEADS * (feed + 1), 0, 0, 0))
                        ys = yraw[:, feed % 2, place, :, :]
                        dve.reciprocal(ws.rden, ys[:, :, VC - 1])
                        ffn_link(dve.tensor_reduce(
                            ws.yn.rearrange("p (h d) -> p h d", d=HD),
                            ys[:, :, 0:VC - 1].rearrange("p h (a d) -> p h d a", a=PARTS), AX.X, ALU.add))
                        yh = ws.yn.rearrange("p (h d) -> p h d", d=HD)
                        dve.tensor_tensor(yh, yh, ws.rden.unsqueeze(2).broadcast_to((128, HEADS, HD)),
                                          ALU.mult).then_inc(y_ready, 1)
                    elif step == "x1":
                        if u is None:
                            dve.wait_ge(xd_in, at(16 * SUBS * (feed + 1), 0, 0, 0))
                        else:
                            dve.wait_ge(xd_in, at(16 * SUBS * feed, 16, u, 16))
                        dve.wait_ge(proj_psum, at(SUBS * feed, 1, place, 1))
                        ffn_link(dve.tensor_tensor(ws.xd, ws.bank[:, 0:DM], ws.xd, ALU.add))
                        ffn_link(dve.bn_stats(ws.stats, ws.xd), alone)
                        ffn_link(dve.bn_aggr(ws.mv, ws.stats))
                        dve.tensor_scalar(ws.ve, ws.mv[:, 1:2], EPS, None, ALU.add).then_inc(x1_var, 1)
                    elif step == "norm":
                        dve.wait_ge(rstd2, at(SUBS * feed, 1, place, 1))
                        dve.tensor_scalar(ws.yn, ws.xd, ws.mv[:, 0:1], ws.rstd,
                                          ALU.subtract, ALU.mult).then_inc(n2, 1)
                    elif step == "route max":
                        dve.wait_ge(route_psum, at(SUBS * feed, 1, place, 1))
                        dve.tensor_reduce(ws.rsm[:, 0:1], ws.bank[:, LORA:LR], AX.X, ALU.max,
                                          negate=True).then_inc(route_max, 1)
                    elif step == "select":
                        dve.wait_ge(route_exp, at(SUBS * feed, 1, place, 1))
                        dve.reciprocal(ws.rsm[:, 2:3], ws.rsm[:, 1:2])
                        ffn_link(dve.max(ws.top8, ws.e16[:, 0:EXPERTS]))
                        ffn_link(dve.tensor_copy(ws.top2[:, 0:2], ws.top8[:, 0:2]), alone)
                        ffn_link(dve.match_replace(out=ws.left, in_to_replace=ws.top2,
                                                   in_values=ws.e16, imm_value=0.0))
                        ffn_link(dve.tensor_tensor(ws.wexp[:, 0, :], ws.e16[:, 0:EXPERTS], ws.left[:, 0:EXPERTS],
                                                   ALU.subtract))
                        dve.tensor_scalar(ws.wexp[:, 1, :], ws.wexp[:, 0, :], ws.rsm[:, 2:3], None, ALU.mult)
                        ffn_link(dve.tensor_scalar(ws.wexp[:, 2, :], ws.wexp[:, 0, :], ws.rsm[:, 2:3], 0.5,
                                                   ALU.mult, ALU.mult))
                        dve.tensor_tensor(
                            ws.g[:, EXPERTS * FF:].rearrange("p (e r) -> p e r", r=RANK),
                            ws.bank[:, 0:LORA].rearrange("p (e r) -> p e r", r=RANK),
                            ws.wexp[:, 1, :].unsqueeze(2).broadcast_to((128, EXPERTS, RANK)),
                            ALU.mult).then_inc(lora_done, 1)
                    elif step == "gated":
                        gg = ws.g[:, 0:EXPERTS * FF]
                        dve.wait_ge(tanh_done, at(SUBS * feed, 1, place, 1))
                        ffn_link(dve.scalar_tensor_tensor(out=gg, in0=gg, scalar=1.0,
                                                          in1=ws.bank[:, 0:EXPERTS * FF],
                                                          op0=ALU.add, op1=ALU.mult))
                        ffn_link(dve.tensor_tensor(gg, ws.bank[:, EXPERTS * FF:GU], gg, ALU.mult))
                        ge = gg.rearrange("p (e f) -> p e f", f=FF)
                        dve.tensor_tensor(
                            ge, ge, ws.wexp[:, 2, :].unsqueeze(2).broadcast_to((128, EXPERTS, FF)),
                            ALU.mult).then_inc(gated, 1)
                    elif step == "out":
                        dve.wait_ge(down_psum, at(SUBS * feed, 1, place, 1))
                        if u is None:
                            dve.wait_ge(res_out, at(16 * SUBS * feed, 0, 0, 0))
                        else:
                            dve.wait_ge(res_out, at(16 * SUBS * feed, 16, u, 0))
                        dve.tensor_tensor(ws.res, ws.bank[:, 0:DM], ws.xd, ALU.add).then_inc(res_ready, 1)
                assert feed is None or k[0] == FFN_LINKS * (1 if u is not None else SUBS), k[0]

            run_stages(dve, body)

        @block.tensor
        def _(pe):
            def transposes(t):
                pe.wait_ge(n1, SUBS * (t + 1))
                for s in range(SUBS):
                    for c in range(CH):
                        ins = pe.transpose(bank[:, c, TOK * s:TOK * (s + 1)], nrm[:, s, 128 * c:128 * (c + 1)],
                                           idf[:, :])
                    ins.then_inc(hT_psum, 1)

            def column_products(m, o):
                for i in range(2):
                    for c in range(CH):
                        for k in range(CH):
                            a = DM * (3 * m + i) + 128 * c
                            ins = pe.matmul(o[:, CH * i + c:CH * i + c + 1], wmod_sb[:, k, a:a + 128],
                                            silc[:, 3, k:k + 1], start=(k == 0), stop=(k == CH - 1))
                return ins

            pe.wait_ge(consts, 16)
            pe.wait_ge(w_mod[0], 16)
            pe.wait_ge(sil_ready, 1)
            column_products(0, bank[:, 7, :]).then_inc(mod_psum, 1)
            transposes(0)
            for t in range(TILES):
                pe.wait_ge(hT_ready, CH * (t + 1))
                if t == 0:
                    pe.wait_ge(w_in, 16)
                for j in range(2 * CH):
                    if t:
                        pe.wait_ge(qk_mid, 2 * CH * (t - 1) + j + 1)
                    for k in range(CH):
                        ins = pe.matmul(bank[:, 2 + j, :], wqkv_sb[:, k, 128 * j:128 * (j + 1)],
                                        hT[:, t % 2, k, :], start=(k == 0), stop=(k == CH - 1))
                    ins.then_inc(qk_psum, 1)
                if t + 1 < TILES:
                    if t == 1:
                        pe.wait_ge(mod_ready, 3)
                    transposes(t + 1)
                for s in range(SUBS):
                    if t == 0 and s == 0:
                        pe.wait_ge(mod_ready, 1)
                    if t and s % 2 == 0:
                        pe.wait_ge(v_mid, 2 * (t - 1) + s // 2 + 1)
                    for k in range(CH):
                        ins = pe.matmul(bank[:, 6 + s // 2, DM * (s % 2):DM * (s % 2 + 1)],
                                        hT[:, t % 2, k, TOK * s:TOK * (s + 1)],
                                        wqkv_sb[:, k, 2 * DM:3 * DM], start=(k == 0), stop=(k == CH - 1))
                    if s % 2:
                        ins.then_inc(v_psum, 1)
                if t == 0:
                    pe.wait_ge(hT_ready, 2 * CH)
                    pe.wait_ge(w_mod[1], 16)
                    pe.wait_ge(sil_ready, 2)
                    for m, vec in enumerate((2, 5)):
                        for k in range(CH):
                            pe.matmul(bank[:, 0, DM * m:DM * (m + 1)], silb[:, k, :],
                                      wmod_sb[:, k, DM * vec:DM * (vec + 1)], start=(k == 0), stop=(k == CH - 1))
                    column_products(1, bank[:, 1, :]).then_inc(mod_psum, 1)
            pe.wait_ge(qk_mid, 2 * CH * TILES)
            pe.wait_ge(v_lo, 2 * TILES)
            pe.wait_ge(mod_ready, 5)
            pe.wait_ge(masks, 32)
            pe.wait_ge(fill, 32)
            pe.wait_ge(made, 5)

            def body(u, steps, tiles, past, shifted):
                attend, scan, feed = tiles
                if scan is not None:
                    pe.wait_ge(k_rows[scan], 16 * len(PAIRS))
                    if scan < 2:
                        pe.wait_ge(q_rows[scan], 16 * (len(PAIRS) + 1))
                    else:
                        pe.wait_ge(q_rows[scan], at(0, 16 * (len(PAIRS) + 1), u, 16 * (len(PAIRS) + 1)))
                for step, i, back in steps:
                    ws, place = (work[0], u) if u is not None else (work[i], i)
                    if step == "scores":
                        t, nc_ = attend, chunks_of(attend)
                        hh, j = i // nc_, i % nc_
                        h = u * HPI + hh
                        if i == 0:
                            pe.wait_ge(shift_in, at(16 * PARTS * SUBS * t, 16 * PARTS, u, 16 * PARTS))
                        pe.wait_ge(exp_done, bank_free(i, t, u))
                        if SCAN <= i < SCORE_BANKS[t] and isinstance(u, int):
                            pe.wait_ge(scan_max, at(maxes_before(t + 1), 0, 0, 0))
                        for kb, sub, col, w in chunk_blocks(t, j):
                            o = bank[:, i % SCORE_BANKS[t], col:col + w]
                            diag = kb >= SUBS * t
                            if diag:
                                pe.matmul(o[:, 0:TOK], idb[:, :], mask_k_sb[:, :],
                                          start=True, stop=False, skip_group_check=True)
                            ins = pe.matmul(o, ka[0:ROW_END, h, TOK * kb:TOK * (kb + 1)],
                                            qa[0:ROW_END, t % 2, h, TOK * sub:TOK * sub + w],
                                            start=not diag, stop=True, skip_group_check=diag)
                        ins.then_inc(scores_psum, 1)
                    elif step in ("mix high", "mix low"):
                        t, at_u, ago, hh, j = mix_place(i, back, tiles, u, past)
                        h = at_u * HPI + (hh - ago * HPI)
                        low = step == "mix low"
                        if low:
                            vector = j in SPLIT_ON_VECTOR[t]
                            per = splits_before(t, chunks_of(t), vector)
                            pe.wait_ge(split_v if vector else split_g,
                                       at(all_splits_before(t, vector), HPI * per, at_u,
                                          hh * per + splits_before(t, j, vector) + 1, ago))
                        else:
                            if j == 0:
                                pe.wait_ge(y_out, at(HEADS * t, HPI, at_u, hh - 1, ago))
                            pe.wait_ge(exp_done, chunk_at(t, at_u, i + 1, ago))
                        for kb, sub, col, w in chunk_blocks(t, j):
                            for q in range(w // TOK):
                                a = col + TOK * q
                                if low:
                                    p = probs_lo[:, i % RING[t], a:a + TOK]
                                else:
                                    p = probs[:, i % RING[t], a:a + TOK].bitcast(bf16)[:, 1::2]
                                s = sub + q
                                ins = pe.matmul(bank[:, MIX + hh % 2, VC * s:VC * (s + 1)], p, vp[:, kb, h, :],
                                                start=(j == 0 and not low and kb == 0 and s == 0),
                                                stop=low and kb == SUBS * t + min(s, 2),
                                                skip_group_check=True)
                        if low:
                            ins.then_inc(mixed, 1)
                    elif step == "scan":
                        r, c = i // (scan + 1), i % (scan + 1)
                        h, s = u * HPI + r // SUBS, r % SUBS
                        w = TILE if c < scan else TOK * (s + 1)
                        pe.wait_ge(scan_max, scan_bank_free(i, scan, u))
                        o = bank[:, SCAN + i % SCAN_BANKS, :]
                        diag = c == scan
                        if diag:
                            pe.matmul(o[:, w - TOK:w], idb[:, :], mask_q_sb[:, :],
                                      start=True, stop=False, skip_group_check=True)
                        pe.matmul(o[:, 0:w], qa[0:ROW_SHIFT, scan % 2, h, TOK * s:TOK * (s + 1)],
                                  ka[0:ROW_SHIFT, h, TILE * c:TILE * c + w],
                                  start=not diag, stop=True, skip_group_check=diag).then_inc(scan_psum, 1)
                    elif step == "shift":
                        t, at_u, ago = shifted
                        pe.wait_ge(shift_own, at(SHIFT_LINKS * SUBS * t, SHIFT_LINKS, at_u, SHIFT_LINKS, ago))
                        if feed is not None:
                            pe.wait_ge(res_ready, at(SUBS * feed, 1, place, 0))
                        pe.wait_ge(shift_sb, at(SUBS * t, 1, at_u, 0, ago))
                        pe.transpose(ws.bank[:, 0:TOK // 2].bitcast(bf16), shift[:, :],
                                     idb[:, :]).then_inc(shift_psum, 1)
                    elif step == "yT":
                        pe.wait_ge(y_ready, at(SUBS * feed, 1, place, 1))
                        if u is None:
                            pe.wait_ge(res_ready, at(SUBS * feed, 0, 0, 0))
                            pe.wait_ge(exp_done, at(chunks_before(TILES), 0, 0, 0))
                        else:
                            pe.wait_ge(res_ready, at(SUBS * feed, 1, u, 0))
                        if shifted is not None:
                            t, at_u, ago = shifted
                            pe.wait_ge(shift_sb, at(SUBS * t, 1, at_u, 1, ago))
                        else:
                            pe.wait_ge(shift_sb, at(SUBS * TILES, 0, 0, 0))
                        for c in range(CH):
                            ins = pe.transpose(ws.bank[:, TOK * c:TOK * (c + 1)],
                                               ws.yn[:, 128 * c:128 * (c + 1)], idf[:, :])
                        ins.then_inc(yT_psum, 1)
                    elif step == "proj":
                        pe.wait_ge(yT_ready, at(SUBS * feed, 1, place, 1))
                        for c in range(CH):
                            ins = pe.matmul(ws.bank[:, 0:DM], ws.tT[:, c, :], wo_sb[:, c, :],
                                            start=(c == 0), stop=(c == CH - 1))
                        ins.then_inc(proj_psum, 1)
                    elif step == "hT":
                        pe.wait_ge(n2, at(SUBS * feed, 1, place, 1))
                        for c in range(CH):
                            ins = pe.transpose(ws.bank[:, TOK * c:TOK * (c + 1)],
                                               ws.yn[:, 128 * c:128 * (c + 1)], idf[:, :])
                        ins.then_inc(n2T_psum, 1)
                    elif step == "route":
                        pe.wait_ge(h2T_ready, at(CH * SUBS * feed, CH, place, CH))
                        for c in range(CH):
                            ins = pe.matmul(ws.bank[:, 0:LR], ws.tT[:, c, :], w_lr_sb[:, c, :],
                                            start=(c == 0), stop=(c == CH - 1))
                        ins.then_inc(route_psum, 1)
                    elif step == "gate":
                        pe.wait_ge(lora_done, at(SUBS * feed, 1, place, 1))
                        for c in range(CH):
                            ins = pe.matmul(ws.bank[:, 0:GU], ws.tT[:, c, :], w_gu_sb[:, c, :],
                                            start=(c == 0), stop=(c == CH - 1))
                        ins.then_inc(gu_psum, 1)
                    elif step == "gT":
                        pe.wait_ge(gated, at(SUBS * feed, 1, place, 1))
                        for c in range(DOWN):
                            ins = pe.transpose(ws.bank[:, TOK * c:TOK * (c + 1)],
                                               ws.g[:, 128 * c:128 * (c + 1)], idf[:, :])
                        ins.then_inc(gT_psum, 1)
                    elif step == "down":
                        pe.wait_ge(gT_ready, at(SUBS * feed, 1, place, 1))
                        for c in range(DOWN):
                            ins = pe.matmul(ws.bank[:, 0:DM], ws.gT[:, c, :], w_down_sb[:, c, :],
                                            start=(c == 0), stop=(c == DOWN - 1))
                        ins.then_inc(down_psum, 1)

            run_stages(pe, body)


def constants():
    bf = np.dtype("bfloat16")
    slopes = np.float32(2.0) ** (np.float32(-8.0) / np.arange(1, HEADS + 1, dtype=np.float32))
    rest, slope_parts = slopes * np.float32(HD ** 0.5), []
    for _ in range(PARTS):
        part = rest.astype(bf).astype(np.float32)
        slope_parts.append(part)
        rest = rest - part
    pos = np.arange(SEQ)
    high, low = (pos // TOK * TOK).astype(np.float32), (pos % TOK).astype(np.float32)
    ones = np.ones(SEQ, np.float32)
    k_side, q_side = [], []
    for part in slope_parts:
        for at_key, at_query, sign in ((high, ones, 1), (ones, high, -1), (low, ones, 1), (ones, low, -1)):
            if sign > 0:
                k_side.append(np.broadcast_to(at_key, (HEADS, SEQ)))
                q_side.append(part[:, None] * ones[None, :])
            else:
                k_side.append(-part[:, None] * ones[None, :])
                q_side.append(np.broadcast_to(at_query, (HEADS, SEQ)))
    k_side += [np.ones((HEADS, SEQ), np.float32)] * PARTS
    i = np.arange(TOK)
    return {
        "alibi_k": np.stack(k_side).astype(bf),
        "alibi_q": np.stack(q_side).astype(bf),
        "ident": np.eye(TOK, dtype=np.float32),
        "mask_q": np.where(i[None, :] > i[:, None], MASKED, 0.0).astype(bf),
        "mask_k": np.where(i[:, None] > i[None, :], MASKED, 0.0).astype(bf),
    }


def kernel(L0_attn_x, L0_attn_W_qkv, L0_attn_W_o, L0_ffn_G, L0_ffn_gate_w, L0_ffn_up_w, L0_ffn_down_w,
           L0_ffn_lora_A, L0_ffn_lora_B, L0_c, L0_wmod):
    import concourse.bacc as _bacc
    from concourse.bass_utils import run_bass_kernel_spmd as _run

    def rows(w):
        w = np.asarray(w)
        return np.ascontiguousarray(w.reshape(-1, 128, w.shape[-1]).transpose(1, 0, 2))

    def by_input(w):
        w = np.asarray(w)
        return w.reshape(-1, w.shape[-1]).T

    def by_feature(w):
        w = np.asarray(w)
        return w.transpose(0, 2, 1).reshape(-1, w.shape[1])

    arrays = {
        "x": np.ascontiguousarray(np.asarray(L0_attn_x).reshape(SEQ, DM)),
        "c_cols": np.ascontiguousarray(np.asarray(L0_c).reshape(CH, 128).T),
        "wmod": rows(L0_wmod),
        "wqkv": rows(L0_attn_W_qkv),
        "wo": rows(L0_attn_W_o),
        "w_lr": rows(np.concatenate([by_input(L0_ffn_lora_A), np.asarray(L0_ffn_G)], axis=1)),
        "w_gu": rows(np.concatenate([by_input(L0_ffn_gate_w), by_input(L0_ffn_up_w)], axis=1)),
        "w_down": rows(np.concatenate([by_feature(L0_ffn_down_w), by_feature(L0_ffn_lora_B)], axis=0)),
    }
    arrays.update(constants())
    nc = _bacc.Bacc("TRN2", target_bir_lowering=False, num_devices=1)
    aps = {n: nc.dram_tensor(n, a.shape, mybir.dt.from_np(a.dtype), kind="ExternalInput").ap()
           for n, a in arrays.items()}
    aps["out"] = nc.dram_tensor("out", (SEQ, DM), mybir.dt.float32, kind="ExternalOutput").ap()
    decoder_layer(nc, **aps)
    r = _run(nc, [arrays], core_ids=[0])
    return r.results[0]["out"].reshape(1, SEQ, DM)
```
